# Optimizing a Trainium2 kernel written in Bass

```python
import numpy as np
import jax
import jax.numpy as jnp

def _softmax(x, axis=-1):
    return jax.nn.softmax(x, axis=axis)

def _gelu(x):
    return jax.nn.gelu(x, approximate=True)

def _silu(x):
    return jax.nn.silu(x)

def _sigmoid(x):
    return jax.nn.sigmoid(x)

def _layernorm(x, axis=-1, eps=1e-05):
    m = jnp.mean(x, axis=axis, keepdims=True)
    v = jnp.var(x, axis=axis, keepdims=True)
    return (x - m) / jnp.sqrt(v + eps)

def _scatter_add(tgt, idx, src, axis=0):
    return tgt.at[idx].add(src)

def _segment_sum(src, seg, n):
    return jax.ops.segment_sum(src, seg, n)
kernel_name = 'mk_adj_ffn_d4_adj_r2_8bd120'

def setup_inputs(seed: int=0):
    np.random.seed(seed)
    _w = jnp.asarray

    def _rec_inputs():
        import jax
        import jax.numpy as jnp
        _gk = jax.random.key(seed)
        x = -0.0002928 + 1 * jax.random.normal(jax.random.fold_in(_gk, 1), (64, 128, 128), jnp.float32)
        _a = jax.random.bernoulli(jax.random.fold_in(_gk, 2), 0.0625, (64, 128, 128))
        _a = jnp.logical_or(_a, jnp.swapaxes(_a, -1, -2))
        _a = jnp.logical_or(_a, jnp.eye(128, dtype=bool))
        adj = _a.astype(jnp.int32)
        return (x, adj)
    x, adj = _rec_inputs()

    def _L0_gnn_setup():
        import jax, jax.numpy as jnp
        import numpy as np
        NEG_INF = -1000000000.0
        LEAKY_SLOPE = 0.2
        key = jax.random.key(seed)
        k1, k2, k3, k4 = jax.random.split(key, 4)
        B, N, D_in, D_out = (8, 1024, 128, 128)
        x = jax.random.normal(k1, (B, N, D_in), dtype=jnp.float32)
        adj_matrix = jax.random.randint(k2, (B, N, N), 0, 2, dtype=jnp.int32)
        W = jax.random.normal(k3, (D_out, D_in), dtype=jnp.float32) / np.sqrt(D_in)
        a = jax.random.normal(k4, (1, 2 * D_out), dtype=jnp.float32) / np.sqrt(2 * D_out)
        return {'x': x, 'adj_matrix': adj_matrix, 'W': W, 'a': a}
    _L0_gnn_all = _L0_gnn_setup()
    _L0_gnn_in = {k: v for k, v in _L0_gnn_all.items() if k in ('W', 'a')}
    del _L0_gnn_all

    def _L0_ffn_setup():
        import jax, jax.numpy as jnp
        import numpy as np
        B, S, D, E, H, K = (4, 2048, 128, 8, 256, 2)
        key = jax.random.key(seed)
        ks = jax.random.split(key, 6)
        x = jax.random.normal(ks[0], (B, S, D), jnp.float32)
        Wg = jax.random.normal(ks[1], (D, E), jnp.float32) * 0.02
        bg = jnp.zeros((E,), jnp.float32)
        W1 = jax.random.normal(ks[2], (E, D, H), jnp.float32) * 0.02
        b1 = jnp.zeros((E, H), jnp.float32)
        W2 = jax.random.normal(ks[3], (E, H, D), jnp.float32) * 0.02
        b2 = jnp.zeros((E, D), jnp.float32)
        return {'x': x, 'Wg': Wg, 'bg': bg, 'W1': W1, 'b1': b1, 'W2': W2, 'b2': b2}
    _L0_ffn_all = _L0_ffn_setup()
    _L0_ffn_in = {k: v for k, v in _L0_ffn_all.items() if k in ('Wg', 'bg', 'W1', 'b1', 'W2', 'b2')}
    del _L0_ffn_all

    def _L1_gnn_setup():
        import jax, jax.numpy as jnp
        import numpy as np
        B, N, D_IN, D_OUT, R = (8, 1024, 128, 128, 4)
        key = jax.random.key(seed)
        k1, k2, k3, k4 = jax.random.split(key, 4)
        x = jax.random.normal(k1, (B, N, D_IN), dtype=jnp.float32)
        adj = jnp.zeros((1,), dtype=jnp.float32)
        relation = jax.random.randint(k2, (B, N, N), 0, R + 1, dtype=jnp.int32)
        weight = jax.random.normal(k3, (R, D_IN, D_OUT), dtype=jnp.float32) * 0.05
        bias = jax.random.normal(k4, (D_OUT,), dtype=jnp.float32) * 0.05
        return {'x': x, 'adj': adj, 'relation': relation, 'weight': weight, 'bias': bias}
    _L1_gnn_all = _L1_gnn_setup()
    _L1_gnn_in = {k: v for k, v in _L1_gnn_all.items() if k in ('adj', 'weight', 'bias')}
    del _L1_gnn_all

    def _L1_ffn_setup():
        import jax, jax.numpy as jnp
        import numpy as np
        E, D, H, TOP_K = (6, 128, 128, 2)
        ROUTER_H = D // 2
        key = jax.random.key(seed)
        ks = jax.random.split(key, 12)
        s = 1.0 / np.sqrt(D)
        sh = 1.0 / np.sqrt(H)
        sr = 1.0 / np.sqrt(ROUTER_H)
        return {'features': jax.random.normal(ks[0], (8, 2048, D), dtype=jnp.float32), 'router_w1': jax.random.uniform(ks[1], (D, ROUTER_H), jnp.float32, -s, s), 'router_b1': jnp.zeros((ROUTER_H,), jnp.float32), 'router_w2': jax.random.uniform(ks[2], (ROUTER_H, E), jnp.float32, -sr, sr), 'router_b2': jnp.zeros((E,), jnp.float32), 'expert_w1': jax.random.uniform(ks[3], (E, D, H), jnp.float32, -s, s), 'expert_b1': jnp.zeros((E, H), jnp.float32), 'expert_w2': jax.random.uniform(ks[4], (E, H, H), jnp.float32, -sh, sh), 'expert_b2': jnp.zeros((E, H), jnp.float32), 'expert_w3': jax.random.uniform(ks[5], (E, H, D), jnp.float32, -sh, sh), 'expert_b3': jnp.zeros((E, D), jnp.float32)}
    _L1_ffn_all = _L1_ffn_setup()
    _L1_ffn_in = {k: v for k, v in _L1_ffn_all.items() if k in ('router_w1', 'router_b1', 'router_w2', 'router_b2', 'expert_w1', 'expert_b1', 'expert_w2', 'expert_b2', 'expert_w3', 'expert_b3')}
    del _L1_ffn_all

    def _L2_gnn_setup():
        import jax, jax.numpy as jnp
        import numpy as np
        DIM = 128
        HEADS = 8
        HEAD_DIM = DIM // HEADS
        DFF = 4 * DIM
        EPS = 1e-05

        def _layernorm(x, g, b):
            m = jnp.mean(x, axis=-1, keepdims=True)
            v = jnp.mean(jnp.square(x - m), axis=-1, keepdims=True)
            return (x - m) * jax.lax.rsqrt(v + EPS) * g + b
        key = jax.random.key(seed)
        ks = jax.random.split(key, 12)
        B, N = (8, 512)
        s = 1.0 / np.sqrt(DIM)
        x = jax.random.normal(ks[0], (B, N, DIM), dtype=jnp.float32)
        adj = jax.random.randint(ks[1], (B, N, N), 0, 2, dtype=jnp.int32)
        return {'x': x, 'adj': adj, 'Wqkv': jax.random.normal(ks[2], (3 * DIM, DIM), jnp.float32) * s, 'bqkv': jnp.zeros((3 * DIM,), jnp.float32), 'Wo': jax.random.normal(ks[3], (DIM, DIM), jnp.float32) * s, 'bo': jnp.zeros((DIM,), jnp.float32), 'ln1_g': jnp.ones((DIM,), jnp.float32), 'ln1_b': jnp.zeros((DIM,), jnp.float32), 'W1': jax.random.normal(ks[4], (DFF, DIM), jnp.float32) * s, 'b1': jnp.zeros((DFF,), jnp.float32), 'W2': jax.random.normal(ks[5], (DIM, DFF), jnp.float32) * (1.0 / np.sqrt(DFF)), 'b2': jnp.zeros((DIM,), jnp.float32), 'ln2_g': jnp.ones((DIM,), jnp.float32), 'ln2_b': jnp.zeros((DIM,), jnp.float32)}
    _L2_gnn_all = _L2_gnn_setup()
    _L2_gnn_in = {k: v for k, v in _L2_gnn_all.items() if k in ('Wqkv', 'bqkv', 'Wo', 'bo', 'ln1_g', 'ln1_b', 'W1', 'b1', 'W2', 'b2', 'ln2_g', 'ln2_b')}
    del _L2_gnn_all

    def _L2_ffn_setup():
        import jax, jax.numpy as jnp
        import numpy as np
        TOP_K = 2
        LN_EPS = 1e-05
        key = jax.random.key(seed)
        ks = jax.random.split(key, 8)
        B, S, D, E, H = (16, 512, 128, 8, 512)
        x = jax.random.normal(ks[0], (B, S, D), dtype=jnp.float32)
        Wr = jax.random.normal(ks[1], (D, E), dtype=jnp.float32) * 0.1
        br = jnp.zeros((E,), dtype=jnp.float32)
        ln_g = jnp.ones((E, D), dtype=jnp.float32)
        ln_b = jnp.zeros((E, D), dtype=jnp.float32)
        W1 = jax.random.normal(ks[2], (E, D, H), dtype=jnp.float32) * (1.0 / np.sqrt(D))
        b1 = jnp.zeros((E, H), dtype=jnp.float32)
        W2 = jax.random.normal(ks[3], (E, H, D), dtype=jnp.float32) * (1.0 / np.sqrt(H))
        b2 = jnp.zeros((E, D), dtype=jnp.float32)
        return {'x': x, 'Wr': Wr, 'br': br, 'ln_g': ln_g, 'ln_b': ln_b, 'W1': W1, 'b1': b1, 'W2': W2, 'b2': b2}
    _L2_ffn_all = _L2_ffn_setup()
    _L2_ffn_in = {k: v for k, v in _L2_ffn_all.items() if k in ('Wr', 'br', 'ln_g', 'ln_b', 'W1', 'b1', 'W2', 'b2')}
    del _L2_ffn_all

    def _L3_gnn_setup():
        import jax, jax.numpy as jnp
        import numpy as np
        NEG_BIG = -9000000000000000.0
        key = jax.random.key(seed)
        k_h, k_adj, k_W, k_a = jax.random.split(key, 4)
        B, N, F_in, F_out = (8, 1024, 128, 128)
        h = jax.random.normal(k_h, (B, N, F_in), dtype=jnp.float32)
        adj = jax.random.randint(k_adj, (B, N, N), 0, 2, dtype=jnp.int32)
        gain = 1.414
        lim_W = gain * np.sqrt(6.0 / (F_in + F_out))
        W = jax.random.uniform(k_W, (F_in, F_out), dtype=jnp.float32, minval=-lim_W, maxval=lim_W)
        lim_a = gain * np.sqrt(6.0 / (2 * F_out + 1))
        a = jax.random.uniform(k_a, (2 * F_out, 1), dtype=jnp.float32, minval=-lim_a, maxval=lim_a)
        return {'h': h, 'adj': adj, 'W': W, 'a': a}
    _L3_gnn_all = _L3_gnn_setup()
    _L3_gnn_in = {k: v for k, v in _L3_gnn_all.items() if k in ('W', 'a')}
    del _L3_gnn_all

    def _L3_ffn_setup():
        import jax, jax.numpy as jnp
        import numpy as np
        B, S, D, H, E, K = (8, 4096, 128, 512, 8, 2)
        key = jax.random.key(seed)
        ks = jax.random.split(key, 7)
        s_in = 1.0 / np.sqrt(D)
        s_hid = 1.0 / np.sqrt(H)
        return {'x': jax.random.normal(ks[0], (B, S, D), dtype=jnp.float32), 'Wg': jax.random.uniform(ks[1], (E, D), jnp.float32, -s_in, s_in), 'bg': jax.random.uniform(ks[2], (E,), jnp.float32, -s_in, s_in), 'W1': jax.random.uniform(ks[3], (E, H, D), jnp.float32, -s_in, s_in), 'b1': jax.random.uniform(ks[4], (E, H), jnp.float32, -s_in, s_in), 'W2': jax.random.uniform(ks[5], (E, D, H), jnp.float32, -s_hid, s_hid), 'b2': jax.random.uniform(ks[6], (E, D), jnp.float32, -s_hid, s_hid)}
    _L3_ffn_all = _L3_ffn_setup()
    _L3_ffn_in = {k: v for k, v in _L3_ffn_all.items() if k in ('Wg', 'bg', 'W1', 'b1', 'W2', 'b2')}
    del _L3_ffn_all
    return {'x': x, 'adj': adj, 'L0_gnn_W': _L0_gnn_in['W'], 'L0_gnn_a': _L0_gnn_in['a'], 'L0_ffn_Wg': _L0_ffn_in['Wg'], 'L0_ffn_bg': _L0_ffn_in['bg'], 'L0_ffn_W1': _L0_ffn_in['W1'], 'L0_ffn_b1': _L0_ffn_in['b1'], 'L0_ffn_W2': _L0_ffn_in['W2'], 'L0_ffn_b2': _L0_ffn_in['b2'], 'L1_gnn_adj': _L1_gnn_in['adj'], 'L1_gnn_weight': _L1_gnn_in['weight'], 'L1_gnn_bias': _L1_gnn_in['bias'], 'L1_ffn_router_w1': _L1_ffn_in['router_w1'], 'L1_ffn_router_b1': _L1_ffn_in['router_b1'], 'L1_ffn_router_w2': _L1_ffn_in['router_w2'], 'L1_ffn_router_b2': _L1_ffn_in['router_b2'], 'L1_ffn_expert_w1': _L1_ffn_in['expert_w1'], 'L1_ffn_expert_b1': _L1_ffn_in['expert_b1'], 'L1_ffn_expert_w2': _L1_ffn_in['expert_w2'], 'L1_ffn_expert_b2': _L1_ffn_in['expert_b2'], 'L1_ffn_expert_w3': _L1_ffn_in['expert_w3'], 'L1_ffn_expert_b3': _L1_ffn_in['expert_b3'], 'L2_gnn_Wqkv': _L2_gnn_in['Wqkv'], 'L2_gnn_bqkv': _L2_gnn_in['bqkv'], 'L2_gnn_Wo': _L2_gnn_in['Wo'], 'L2_gnn_bo': _L2_gnn_in['bo'], 'L2_gnn_ln1_g': _L2_gnn_in['ln1_g'], 'L2_gnn_ln1_b': _L2_gnn_in['ln1_b'], 'L2_gnn_W1': _L2_gnn_in['W1'], 'L2_gnn_b1': _L2_gnn_in['b1'], 'L2_gnn_W2': _L2_gnn_in['W2'], 'L2_gnn_b2': _L2_gnn_in['b2'], 'L2_gnn_ln2_g': _L2_gnn_in['ln2_g'], 'L2_gnn_ln2_b': _L2_gnn_in['ln2_b'], 'L2_ffn_Wr': _L2_ffn_in['Wr'], 'L2_ffn_br': _L2_ffn_in['br'], 'L2_ffn_ln_g': _L2_ffn_in['ln_g'], 'L2_ffn_ln_b': _L2_ffn_in['ln_b'], 'L2_ffn_W1': _L2_ffn_in['W1'], 'L2_ffn_b1': _L2_ffn_in['b1'], 'L2_ffn_W2': _L2_ffn_in['W2'], 'L2_ffn_b2': _L2_ffn_in['b2'], 'L3_gnn_W': _L3_gnn_in['W'], 'L3_gnn_a': _L3_gnn_in['a'], 'L3_ffn_Wg': _L3_ffn_in['Wg'], 'L3_ffn_bg': _L3_ffn_in['bg'], 'L3_ffn_W1': _L3_ffn_in['W1'], 'L3_ffn_b1': _L3_ffn_in['b1'], 'L3_ffn_W2': _L3_ffn_in['W2'], 'L3_ffn_b2': _L3_ffn_in['b2']}

def reference(x, adj, L0_gnn_W, L0_gnn_a, L0_ffn_Wg, L0_ffn_bg, L0_ffn_W1, L0_ffn_b1, L0_ffn_W2, L0_ffn_b2, L1_gnn_adj, L1_gnn_weight, L1_gnn_bias, L1_ffn_router_w1, L1_ffn_router_b1, L1_ffn_router_w2, L1_ffn_router_b2, L1_ffn_expert_w1, L1_ffn_expert_b1, L1_ffn_expert_w2, L1_ffn_expert_b2, L1_ffn_expert_w3, L1_ffn_expert_b3, L2_gnn_Wqkv, L2_gnn_bqkv, L2_gnn_Wo, L2_gnn_bo, L2_gnn_ln1_g, L2_gnn_ln1_b, L2_gnn_W1, L2_gnn_b1, L2_gnn_W2, L2_gnn_b2, L2_gnn_ln2_g, L2_gnn_ln2_b, L2_ffn_Wr, L2_ffn_br, L2_ffn_ln_g, L2_ffn_ln_b, L2_ffn_W1, L2_ffn_b1, L2_ffn_W2, L2_ffn_b2, L3_gnn_W, L3_gnn_a, L3_ffn_Wg, L3_ffn_bg, L3_ffn_W1, L3_ffn_b1, L3_ffn_W2, L3_ffn_b2):
    import jax
    import jax.numpy as jnp

    def _L0_gnn_ref(x, adj_matrix, W, a):
        import jax, jax.numpy as jnp
        import numpy as np
        NEG_INF = -1000000000.0
        LEAKY_SLOPE = 0.2
        h = jnp.einsum('bnd,od->bno', x, W)
        D = h.shape[-1]
        a_left, a_right = (a[0, :D], a[0, D:])
        e = (h @ a_left)[:, :, None] + (h @ a_right)[:, None, :]
        e = jnp.where(e > 0, e, LEAKY_SLOPE * e)
        e = jnp.where(adj_matrix == 0, NEG_INF, e)
        alpha = jax.nn.softmax(e, axis=-1)
        return jnp.einsum('bij,bjd->bid', alpha, h)

    def _L0_ffn_ref(x, Wg, bg, W1, b1, W2, b2):
        import jax, jax.numpy as jnp
        import numpy as np
        B, S, D, E, H, K = (4, 2048, 128, 8, 256, 2)
        Bv, Sv, Dv = x.shape
        gate_scores = x @ Wg + bg
        _, idx = jax.lax.top_k(gate_scores, K)
        mask = jax.nn.one_hot(idx, E, dtype=x.dtype).sum(axis=-2)
        xf = x.reshape(-1, Dv)
        mf = mask.reshape(-1, E)
        h = jax.nn.gelu(jnp.einsum('td,edh->teh', xf, W1) + b1[None], approximate=False)
        y = jnp.einsum('teh,ehd->ted', h, W2) + b2[None]
        out = jnp.einsum('ted,te->td', y, mf)
        return out.reshape(Bv, Sv, Dv)

    def _L1_gnn_ref(x, adj, relation, weight, bias):
        import jax, jax.numpy as jnp
        import numpy as np
        B, N, D_IN, D_OUT, R = (8, 1024, 128, 128, 4)
        rel_ids = jnp.arange(1, weight.shape[0] + 1, dtype=relation.dtype)
        masks = (relation[None] == rel_ids[:, None, None, None]).astype(x.dtype)
        h = jnp.einsum('rbnm,bmd->rbnd', masks, x)
        y = jnp.einsum('rbnd,rdo->bno', h, weight)
        return y + bias

    def _L1_ffn_ref(features, router_w1, router_b1, router_w2, router_b2, expert_w1, expert_b1, expert_w2, expert_b2, expert_w3, expert_b3):
        import jax, jax.numpy as jnp
        import numpy as np
        E, D, H, TOP_K = (6, 128, 128, 2)
        ROUTER_H = D // 2
        rh = jax.nn.relu(features @ router_w1 + router_b1)
        expert_logits = jax.nn.softmax(rh @ router_w2 + router_b2, axis=-1)
        top_w, top_i = jax.lax.top_k(expert_logits, TOP_K)
        routing_weights = jax.nn.softmax(top_w, axis=-1)
        h1 = jax.nn.relu(jnp.einsum('bsd,edh->bseh', features, expert_w1) + expert_b1)
        h2 = jax.nn.relu(jnp.einsum('bseh,ehf->bsef', h1, expert_w2) + expert_b2)
        expert_out = jnp.einsum('bsef,efo->bseo', h2, expert_w3) + expert_b3
        sel = jnp.take_along_axis(expert_out, top_i[:, :, :, None], axis=2)
        combined = jnp.sum(sel * routing_weights[..., None], axis=2)
        return combined

    def _L2_gnn_ref(x, adj, Wqkv, bqkv, Wo, bo, ln1_g, ln1_b, W1, b1, W2, b2, ln2_g, ln2_b):
        import jax, jax.numpy as jnp
        import numpy as np
        DIM = 128
        HEADS = 8
        HEAD_DIM = DIM // HEADS
        DFF = 4 * DIM
        EPS = 1e-05

        def _layernorm(x, g, b):
            m = jnp.mean(x, axis=-1, keepdims=True)
            v = jnp.mean(jnp.square(x - m), axis=-1, keepdims=True)
            return (x - m) * jax.lax.rsqrt(v + EPS) * g + b
        B, N, _ = x.shape
        eye = jnp.eye(N, dtype=bool)[None]
        allowed = (adj > 0) | (jnp.swapaxes(adj, 1, 2) > 0) | eye
        qkv = x @ Wqkv.T + bqkv
        q, k, v = jnp.split(qkv, 3, axis=-1)

        def heads(t):
            return t.reshape(B, N, HEADS, HEAD_DIM).transpose(0, 2, 1, 3)
        q, k, v = (heads(q), heads(k), heads(v))
        scale = 1.0 / np.sqrt(HEAD_DIM)
        scores = jnp.einsum('bhqd,bhkd->bhqk', q * scale, k)
        scores = jnp.where(allowed[:, None], scores, -jnp.inf)
        attn = jax.nn.softmax(scores, axis=-1)
        ctx = jnp.einsum('bhqk,bhkd->bhqd', attn, v)
        ctx = ctx.transpose(0, 2, 1, 3).reshape(B, N, DIM)
        attn_out = ctx @ Wo.T + bo
        x = _layernorm(x + attn_out, ln1_g, ln1_b)
        ff = jax.nn.relu(x @ W1.T + b1) @ W2.T + b2
        x = _layernorm(x + ff, ln2_g, ln2_b)
        return x

    def _L2_ffn_ref(x, Wr, br, ln_g, ln_b, W1, b1, W2, b2):
        import jax, jax.numpy as jnp
        import numpy as np
        TOP_K = 2
        LN_EPS = 1e-05
        B, S, D = x.shape
        N = B * S
        xt = x.reshape(N, D)
        logits = xt @ Wr + br
        probs = jax.nn.softmax(logits, axis=-1)
        top_p, top_idx = jax.lax.top_k(probs, TOP_K)
        weights = top_p / top_p.sum(axis=-1, keepdims=True)
        mu = xt.mean(axis=-1, keepdims=True)
        var = ((xt - mu) ** 2).mean(axis=-1, keepdims=True)
        xn = (xt - mu) * jax.lax.rsqrt(var + LN_EPS)
        xe = xn[None, :, :] * ln_g[:, None, :] + ln_b[:, None, :]
        h = jax.nn.gelu(jnp.einsum('end,edh->enh', xe, W1) + b1[:, None, :], approximate=False)
        y = jnp.einsum('enh,ehd->end', h, W2) + b2[:, None, :]
        y_tok = jnp.transpose(y, (1, 0, 2))
        sel = jnp.take_along_axis(y_tok, top_idx[:, :, None], axis=1)
        out = (weights[:, :, None] * sel).sum(axis=1)
        return out.reshape(B, S, D)

    def _L3_gnn_ref(h, adj, W, a):
        import jax, jax.numpy as jnp
        import numpy as np
        NEG_BIG = -9000000000000000.0
        F_out = W.shape[1]
        Wh = jnp.matmul(h, W)
        a1 = a[:F_out, 0]
        a2 = a[F_out:, 0]
        e = (Wh @ a1)[:, :, None] + (Wh @ a2)[:, None, :]
        masked = jnp.where(adj > 0, e, jnp.float32(NEG_BIG))
        attention = jax.nn.softmax(masked, axis=-1)
        h_prime = jnp.matmul(attention, Wh)
        return jax.nn.elu(h_prime)

    def _L3_ffn_ref(x, Wg, bg, W1, b1, W2, b2):
        import jax, jax.numpy as jnp
        import numpy as np
        B, S, D, H, E, K = (8, 4096, 128, 512, 8, 2)
        gate_scores = jnp.einsum('bsd,ed->bse', x, Wg) + bg
        topk_scores, topk_idx = jax.lax.top_k(gate_scores, K)
        topk_probs = jax.nn.softmax(topk_scores, axis=-1)
        combine = jnp.sum(topk_probs[..., None] * jax.nn.one_hot(topk_idx, E, dtype=x.dtype), axis=-2)
        out = jnp.zeros_like(x)
        for e in range(E):
            h = jax.nn.relu(jnp.einsum('bsd,hd->bsh', x, W1[e]) + b1[e])
            y = jnp.einsum('bsh,dh->bsd', h, W2[e]) + b2[e]
            out = out + combine[..., e:e + 1] * y
        return out
    x = x + _L0_gnn_ref(_layernorm(x, axis=-1), adj, L0_gnn_W, L0_gnn_a)
    x = x + _L0_ffn_ref(_layernorm(x, axis=-1), L0_ffn_Wg, L0_ffn_bg, L0_ffn_W1, L0_ffn_b1, L0_ffn_W2, L0_ffn_b2)
    x = x + _L1_gnn_ref(_layernorm(x, axis=-1), L1_gnn_adj, adj, L1_gnn_weight, L1_gnn_bias)
    x = x + _L1_ffn_ref(_layernorm(x, axis=-1), L1_ffn_router_w1, L1_ffn_router_b1, L1_ffn_router_w2, L1_ffn_router_b2, L1_ffn_expert_w1, L1_ffn_expert_b1, L1_ffn_expert_w2, L1_ffn_expert_b2, L1_ffn_expert_w3, L1_ffn_expert_b3)
    x = x + _L2_gnn_ref(_layernorm(x, axis=-1), adj, L2_gnn_Wqkv, L2_gnn_bqkv, L2_gnn_Wo, L2_gnn_bo, L2_gnn_ln1_g, L2_gnn_ln1_b, L2_gnn_W1, L2_gnn_b1, L2_gnn_W2, L2_gnn_b2, L2_gnn_ln2_g, L2_gnn_ln2_b)
    x = x + _L2_ffn_ref(_layernorm(x, axis=-1), L2_ffn_Wr, L2_ffn_br, L2_ffn_ln_g, L2_ffn_ln_b, L2_ffn_W1, L2_ffn_b1, L2_ffn_W2, L2_ffn_b2)
    x = x + _L3_gnn_ref(_layernorm(x, axis=-1), adj, L3_gnn_W, L3_gnn_a)
    x = x + _L3_ffn_ref(_layernorm(x, axis=-1), L3_ffn_Wg, L3_ffn_bg, L3_ffn_W1, L3_ffn_b1, L3_ffn_W2, L3_ffn_b2)
    return x

_drawn_inputs = setup_inputs


def setup_inputs(seed=0):
    import zlib

    import numpy as np

    out = dict(_drawn_inputs(seed))
    spreads = {'L0_ffn_bg': (0.0, 0.1),
     'L0_ffn_b1': (0.0, 0.1),
     'L0_ffn_b2': (0.0, 0.1),
     'L1_ffn_router_b1': (0.0, 0.459),
     'L1_ffn_router_b2': (0.0, 0.546),
     'L1_ffn_expert_b1': (0.0, 0.8),
     'L1_ffn_expert_b2': (0.0, 0.637),
     'L1_ffn_expert_b3': (0.0, 0.307),
     'L2_gnn_bqkv': (0.0, 0.306),
     'L2_gnn_bo': (0.0, 0.325),
     'L2_gnn_ln1_g': (1.0, 0.2),
     'L2_gnn_ln1_b': (0.0, 0.335),
     'L2_gnn_b1': (0.0, 0.447),
     'L2_gnn_b2': (0.0, 0.337),
     'L2_gnn_ln2_g': (1.0, 0.2),
     'L2_gnn_ln2_b': (0.0, 0.289),
     'L2_ffn_br': (0.0, 0.293),
     'L2_ffn_ln_g': (1.0, 0.6),
     'L2_ffn_ln_b': (0.0, 0.603),
     'L2_ffn_b1': (0.0, 0.643),
     'L2_ffn_b2': (0.0, 0.438)}
    factors = {'L1_gnn_bias': 2.833,
     'L1_ffn_expert_w1': 3.025,
     'L1_ffn_expert_w2': 2.732,
     'L3_ffn_bg': 5.787,
     'L3_ffn_b1': 8.0,
     'L3_ffn_b2': 8.0}
    for name, (base, spread) in spreads.items():
        noise = np.random.default_rng([zlib.crc32(name.encode()), seed]).standard_normal(out[name].shape)
        drawn = base * np.exp(spread * noise) if base else spread * noise
        out[name] = jnp.asarray(drawn.astype(out[name].dtype))
    for name, factor in factors.items():
        out[name] = (out[name] * factor).astype(out[name].dtype)
    return out
```

```python
from contextlib import ExitStack

import numpy as np
import concourse.bass as bass
from concourse import mybir

F32 = mybir.dt.float32
F32R = mybir.dt.float32r
BF16 = mybir.dt.bfloat16
I32 = mybir.dt.int32
ALU = mybir.AluOpType
ACT = mybir.ActivationFunctionType
AX = mybir.AxisListType.X

P = 128
GRAPHS = 64
PER_GROUP = 4
GROUPS = GRAPHS // PER_GROUP
TOK = PER_GROUP * P
LAYERS = 4
EXPERTS = [8, 6, 8, 8]
BLOCKS = [2, 1, 4, 4]
JOBS = [16, 12, 32, 32]
SLOTS = EXPERTS
HB = 4
EPS = 1e-5
L1_FIRST = [0, 1, 4, 6, 8, 10]
L1_SECOND = [2, 3, 5, 7, 9, 11]
EXPS = slice(256, 292)
ROUTE_1, ROUTE_2, ROUTE_3 = 15, 18, 13
MASKED = -float(2 ** 60)
BARRED = -float(2 ** 100)
RELATIONS = 4
HEADS = 8
HD = P // HEADS


class Signal:

    def __init__(self, sem, per):
        self.sem, self.per = sem, per

    def before(self, layer, g):
        return GROUPS * sum(self.per[:layer]) + g * self.per[layer]

    def at(self, layer, g, k=None):
        return self.before(layer, g) + (self.per[layer] if k is None else k)


class Count:

    def __init__(self, sig, layer, g, start=0):
        self.sem, self.first, self.n = sig.sem, sig.before(layer, g), start
        self.all = sig.per[layer]

    def one(self):
        self.n += 1
        return 1

    def value(self):
        return self.first + self.n

    def full(self):
        assert self.n == self.all, (self.n, self.all)


def due(value):
    return not isinstance(value, int) or value > 0


def span(start, size):
    return slice(start, start + size) if isinstance(start, int) else bass.ds(start, size)


COLS = [("l0_b1", 16), ("l0_b2", 8), ("l0_a", 2), ("l1_rb1", 1), ("l1_b1", 6), ("l1_b2", 6),
        ("l1_b3", 6), ("l2_bq", 1), ("l2_bk", 1), ("l2_mb1", 4), ("l2_b1", 32), ("l2_b2", 8),
        ("l2_lng", 8), ("l2_lnb", 8), ("l3_a", 2), ("l3_b1", 32), ("l3_b2", 8)]
ROWS = [("l0_bg", 8), ("l1_bg", 6), ("l2_bg", 8), ("l3_bg", 8), ("l1_bias", P), ("l2_bv", P),
        ("l2_bo", P), ("l2_g1", P), ("l2_c1", P), ("l2_mb2", P), ("l2_g2", P), ("l2_c2", P)]
MATS = [("l0_wT", P), ("l0_w", P), ("l0_wg", 8), ("l1_w", RELATIONS * P), ("l1_rw1", 64),
        ("l1_rw2", 6), ("l2_wq", P), ("l2_wk", P), ("l2_wv", P), ("l2_wo", P), ("l2_w1", 4 * P),
        ("l2_w2", 4 * P), ("l2_wg", 8), ("l3_w", P), ("l3_wT", P), ("l3_wg", 8)]


def places(table):
    at, out = 0, {}
    for name, n in table:
        out[name] = (at, n)
        at += n
    return out, at


COL_AT, N_COLS = places(COLS)
ROW_AT, N_ROWS = places(ROWS)
MAT_AT, N_MATS = places(MATS)

PREP_STEPS = {
    0: [(0, "p_norm"), (0, "p_apply"), (1, "p_turn"), (2, "p_split"), (2, "p_logits"), (3, "p_route"), (5, "p_gates")],
    1: [(0, "p_norm"), (0, "p_apply"), (1, "p_turn"), (2, "p_split"), (2, "p_router"), (2, "p_logits"), (3, "p_route"),
        (5, "p_gates")],
    2: [(0, "p_norm"), (0, "p_apply"), (1, "p_turn"), (1, "p_norm2"), (1, "p_apply2"), (2, "p_logits"),
        (2, "p_route"), (4, "p_turn2"), (5, "p_split"), (6, "p_gates")],
    3: [(0, "p_norm"), (0, "p_apply"), (1, "p_turn"), (2, "p_split"), (2, "p_logits"), (3, "p_route"), (5, "p_gates")],
}
ATTEND = [(0, "g_norm"), (0, "g_apply"), (1, "g_turn"), (2, "g_scores"), (3, "g_center"), (4, "g_exp"),
          (5, "g_turn_p"), (6, "g_mix"), (7, "g_add")]
GNN_STEPS = {
    0: ATTEND,
    1: [(0, "g_norm"), (0, "g_apply"), (1, "g_rel0"), (2, "g_rel1"), (3, "g_mix"), (4, "g_add")],
    3: ATTEND,
}


TRANSFORMER = [
    ("t_mix", -1, 3), ("t_mlp1", -2, 0), ("t_norm", 1, 0), ("t_pow", 1, 0), ("t_apply", 1, 0),
    ("t_turn_p", 0, 0), ("t_keys", 0, 2), ("t_scores", 0, 1), ("t_turn_c", -1, 0),
    ("t_mix", 0, 0), ("t_mlp1", -2, 1), ("t_out", -1, 0), ("t_pow", -1, 1), ("t_turn_p", 0, 1),
    ("t_keys", 0, 3), ("t_scores", 0, 2), ("t_turn", 1, 0),
    ("t_mix", 0, 1), ("t_project", 1, 0), ("t_norm1", -1, 0), ("t_turn_p", 0, 2), ("t_keys", 1, 0),
    ("t_scores", 0, 3),
    ("t_mix", 0, 2), ("t_mlp2", -2, 0), ("t_pow", -2, 2), ("t_mask", 1, 0), ("t_queries", 1, 0),
    ("t_turn_n", -1, 0), ("t_norm2", -2, 0), ("t_keys", 1, 1), ("t_turn_p", 0, 3), ("t_scores", 1, 0),
]


def steps_at(table, slot):
    return [name for at, name in table if at == slot]


def side_order(layer, g, slot):
    last = isinstance(g, int) and g >= GROUPS - 2
    out = []
    nxt = (layer, g + 1) if not (isinstance(g, int) and g == GROUPS - 1) else (layer + 1, 0)
    if nxt[0] < LAYERS and nxt[0] != 2 or nxt[0] == layer:
        out += [(name, *nxt) for name in steps_at(PREP_STEPS[nxt[0]], slot)]
    target = (layer, g + 2) if not last else (layer + 1, g - (GROUPS - 2))
    if target[0] in GNN_STEPS:
        out += [(name, *target) for name in steps_at(GNN_STEPS[target[0]], slot)]
    if layer == 1 and isinstance(g, int) and g == GROUPS - 1:
        out += [("w2_bias", 2, 0)] * (slot == 2) + [("w2_split", 2, slot - 3)] * (slot >= 3)
    if layer == 2 and isinstance(g, int) and g == 0:
        out += [("w3_split", 3, slot - 4)] * (slot >= 4)
    out.sort(key=lambda step: "apply" in step[0])
    return out


def build(nc, x, adj, adjT, mats, cols, rows, l0_w1, l0_w2, l1_w1, l1_w2, l1_w3,
          l2_w1, l2_w2, l3_w1, l3_w2, out, until=LAYERS):
    with ExitStack() as ctx:
        def sb(name, shape, dt=F32):
            return ctx.enter_context(nc.sbuf_tensor(name, shape, dt))

        def ps(name, banks=1):
            return ctx.enter_context(nc.psum_tensor(name, [P, banks * TOK], F32))

        def signal(name, *per):
            return Signal(ctx.enter_context(nc.semaphore(name)), list(per))

        def sem(name):
            return ctx.enter_context(nc.semaphore(name))

        X = sb("X", [P, GRAPHS * P])
        ADJ = sb("ADJ", [P, 2 * TOK], I32)
        MATW = sb("MATW", [P, N_MATS])
        COLW = sb("COLW", [P, N_COLS])
        ROWW = sb("ROWW", [P, N_ROWS])
        WA_R = sb("WA_R", [P, 8192], F32R)
        WA_F = sb("WA_F", [P, 4096])
        WB_R = sb("WB_R", [P, 8192], F32R)
        WB_F = sb("WB_F", [P, 4096])
        V = sb("V", [P, 4 * P])
        IDF = sb("IDF", [P, P])
        IDB = sb("IDB", [P, P], BF16)
        SEL = sb("SEL", [24, 8 * P], BF16)
        IOTA = sb("IOTA", [P, 8])
        POW = sb("POW", [P, 4])
        HM = sb("HM", [P, HEADS])
        LNB1 = sb("LNB1", [P, 32])
        H = sb("H", [P, HB * TOK])
        XH = sb("XH", [P, 2 * TOK], F32R)
        XL = sb("XL", [P, 2 * TOK], F32R)
        GT = sb("GT", [24, 2 * TOK], BF16)
        WORK = sb("WORK", [P, 8 * TOK])
        GS = WORK[:, 0:2 * TOK]
        T = WORK[:, 2 * TOK:4 * TOK]
        ACC = WORK[:, 4 * TOK:5 * TOK]
        PT = WORK[:, 5 * TOK:6 * TOK]
        PX = WORK[:, 6 * TOK:7 * TOK]
        PX2 = WORK[:, 7 * TOK:8 * TOK]
        ST = sb("ST", [P, 4 * 6])
        MV = sb("MV", [P, 4 * 2])
        RS = sb("RS", [P, 4])
        GST = sb("GST", [P, 4 * 6])
        GMV = sb("GMV", [P, 4 * 2])
        GRS = sb("GRS", [P, 4])
        RT = sb("RT", [P, 12 * 32])
        RV = sb("RV", [P, 12 * 4])
        GB3 = sb("GB3", [P, 4 * 24], BF16)
        PEN = sb("PEN", [P, TOK], BF16)
        NEB = sb("NEB", [P, P], BF16)
        BQ4 = sb("BQ4", [P, 1])
        SCR = sb("SCR", [P, 4608])

        def col(name, i=0):
            return COLW[:, COL_AT[name][0] + i:COL_AT[name][0] + i + 1]

        def row(name):
            return ROWW[:, ROW_AT[name][0]:ROW_AT[name][0] + ROW_AT[name][1]]

        def mat(name, i=0, n=None):
            at, width = MAT_AT[name]
            return MATW[:, at + i:at + i + (n or width)]

        def x_at(g):
            return X[:, span(g * TOK, TOK)]

        def half(t, g, rows_=P):
            return t[0:rows_, span((g % 2) * TOK, TOK)]

        def graphs(ap, n=P):
            return ap.rearrange("p (b n) -> p b n", n=n)

        W1 = {0: (WA_R, 0, 2048), 1: (WA_R, 4096, 768), 2: (WB_R, 0, 4096), 3: (WA_R, 0, 4096)}
        W2 = {0: (WA_F, 0), 1: (WA_F, 2048), 2: (WB_F, 0), 3: (WA_F, 0)}
        ZZ, YY, QQ = ps("ZZ", 2), ps("YY", 2), ps("QQ", 2)
        Z = [ZZ[:, 0:TOK], ZZ[:, TOK:2 * TOK]]
        Y = [YY[:, 0:TOK], YY[:, TOK:2 * TOK]]
        GB, PA = QQ[:, 0:TOK], QQ[:, TOK:2 * TOK]
        PB, PC = ps("PB"), ps("PC")

        x_first, x_rest = sem("x_first"), sem("x_rest")
        small_in, w_in, w2_in = sem("small_in"), sem("w_in"), sem("w2_in")
        stage_in = sem("stage_in")
        consts, consts2 = sem("consts"), sem("consts2")
        w_split = sem("w_split")
        v_mm, v_done = sem("v_mm"), sem("v_done")
        stored = sem("stored")
        adj_in = signal("adj_in", 16, 16, 32, 16)
        z_full = signal("z_full", *JOBS)
        h_done = signal("h_done", *JOBS)
        y_full = signal("y_full", *EXPERTS)
        g_full = signal("g_full", *EXPERTS)
        gs_done = signal("gs_done", *EXPERTS)
        comb = signal("comb", *EXPERTS)
        acc_done = signal("acc_done", *[e - 1 for e in EXPERTS])
        tail_tr = signal("tail_tr", 1, 1, 1, 1)
        tail_x = signal("tail_x", 1, 1, 1, 1)
        p_ln = signal("p_ln", 13, 13, 26, 13)
        p_rs = signal("p_rs", 1, 1, 2, 1)
        g_rs = signal("g_rs", 1, 1, 0, 1)
        p_tr = signal("p_tr", 1, 1, 2, 1)
        p_ev = signal("p_ev", 1, 1, 2, 1)
        p_sp = signal("p_sp", 2, 2, 2, 2)
        p_r1 = signal("p_r1", 0, 1, 0, 0)
        p_rh = signal("p_rh", 0, 1, 0, 0)
        p_lg = signal("p_lg", 1, 1, 1, 1)
        p_dv = signal("p_dv", 17, 28, 23, 23)
        p_ex = signal("p_ex", 0, 2, 1, 1)
        p_gt = signal("p_gt", 1, 1, 1, 1)
        p_ge = signal("p_ge", 1, 1, 1, 1)
        g_ln = signal("g_ln", 13, 13, 0, 13)
        g_pen = signal("g_pen", 1, 4, 0, 1)
        g_tr = signal("g_tr", 1, 2, 0, 1)
        g_ev = signal("g_ev", 1, 4, 0, 1)
        g_sc = signal("g_sc", 1, 0, 0, 1)
        g_se = signal("g_se", 2, 0, 0, 1)
        g_ce = signal("g_ce", 3, 0, 0, 2)
        g_ex = signal("g_ex", 1, 0, 0, 1)
        g_pt = signal("g_pt", 1, 0, 0, 1)
        g_su = signal("g_su", 2, 0, 0, 2)
        g_pe = signal("g_pe", 1, 0, 0, 1)
        g_mx = signal("g_mx", 1, 1, 0, 1)
        g_ad = signal("g_ad", 2, 2, 0, 4)
        g_el = signal("g_el", 0, 0, 0, 1)

        t_ln = signal("t_ln", 0, 0, 14, 0)
        t_rw = [signal("t_rw0", 0, 0, 1, 0), signal("t_rw1", 0, 0, 1, 0), signal("t_rw2", 0, 0, 1, 0)]
        t_tr = signal("t_tr", 0, 0, 1, 0)
        t_ut = signal("t_ut", 0, 0, 1, 0)
        t_qkv = signal("t_qkv", 0, 0, 3, 0)
        t_kt = signal("t_kt", 0, 0, 1, 0)
        t_qt = signal("t_qt", 0, 0, 1, 0)
        t_ve = signal("t_ve", 0, 0, 1, 0)
        t_pen = signal("t_pen", 0, 0, 2, 0)
        t_km = signal("t_km", 0, 0, 4, 0)
        t_sc = signal("t_sc", 0, 0, 4, 0)
        t_ce = signal("t_ce", 0, 0, 8, 0)
        t_ex = signal("t_ex", 0, 0, 4, 0)
        t_tp = signal("t_tp", 0, 0, 4, 0)
        t_pe = signal("t_pe", 0, 0, 4, 0)
        t_pv = signal("t_pv", 0, 0, 4, 0)
        t_cx = signal("t_cx", 0, 0, 8, 0)
        t_ct = signal("t_ct", 0, 0, 1, 0)
        t_cv = signal("t_cv", 0, 0, 1, 0)
        t_wo = signal("t_wo", 0, 0, 1, 0)
        t_n1 = signal("t_n1", 0, 0, 18, 0)
        t_t1 = signal("t_t1", 0, 0, 1, 0)
        t_nt = signal("t_nt", 0, 0, 1, 0)
        t_m1 = signal("t_m1", 0, 0, 4, 0)
        t_mh = signal("t_mh", 0, 0, 4, 0)
        t_m2 = signal("t_m2", 0, 0, 1, 0)
        t_x = signal("t_x", 0, 0, 17, 0)
        w_bias, l2_consts = sem("w_bias"), sem("l2_consts")

        TE = SCR[:, 0:1024]
        TPT = SCR[:, 1024:2048]
        TKM = [SCR[:, 2048:3072], SCR[:, 3072:4096]]
        TQT = SCR[:, 4096:4608]
        TU_RING, TKT_RING, TNB_RING = WA_F[:, 0:2048], WA_F[:, 2048:3072], WA_F[:, 3072:4096]
        TVE = WORK[:, 0:1088]
        TC = WORK[:, 1088:1600]
        TT = WORK[:, 1600:2112]
        TNT = WORK[:, 2112:2624]
        TU = WORK[:, 2624:3136]
        TN1 = WORK[:, 3136:3648]
        TM = WORK[:, 3648:3904].bitcast(BF16)
        TR2 = TU
        ST2, MV2 = RT[:, 0:24], RT[:, 24:32]
        TRC = RV[:, 0:8]
        VE_ROW = HEADS * (HD + 1)

        GXN = SCR[:, 0:512]
        GXT = SCR[:, 512:1024]
        GH = SCR[:, 1024:1536]
        GZ = SCR[:, 1536:2048]
        GE = SCR[:, 2048:2560]
        GP = SCR[:, 2560:3072]
        GPT = SCR[:, 3072:3584]
        GR = SCR[:, 3584:3600]
        GM = SCR[:, 512:2560]
        GHT = SCR[:, 2560:4608]

        block = ctx.enter_context(nc.Block())
        layers = range(until)

        class Walk:

            def __init__(self, eng, slot, tail, steps, begin, ahead):
                self.eng, self.slot, self.tail, self.steps = eng, slot, tail, steps
                self.begin, self.ahead = begin, ahead

            def group(self, layer, g):
                if layer == 1 and isinstance(g, int) and g == 0:
                    self.slot(layer, g, -1)
                for s in range(SLOTS[layer]):
                    self.slot(layer, g, s)
                    if s == 0 and not (layer == 0 and isinstance(g, int) and g == 0) \
                            and not (layer == 2 and isinstance(g, int) and g == 0):
                        self.tail(*((layer, g - 1) if not (isinstance(g, int) and g == 0)
                                    else (layer - 1, GROUPS - 1)))
                    for name, la, gr in side_order(layer, g, s):
                        if la < until and name in self.steps:
                            self.steps[name](la, gr)

            def alone(self, table, layer, g):
                for _, name in table[layer]:
                    if name in self.steps:
                        self.steps[name](layer, g)

            def transformer(self, g):
                for name, ahead, b in TRANSFORMER:
                    if not isinstance(g, int) or 0 <= g + ahead < GROUPS:
                        if name in self.steps:
                            self.steps[name](g + ahead, b)

            def run(self):
                self.begin()
                self.alone(GNN_STEPS, 0, 0)
                self.alone(PREP_STEPS, 0, 0)
                self.alone(GNN_STEPS, 0, 1)
                self.ahead(0)
                for layer in layers:
                    if layer == 2:
                        self.tail(1, GROUPS - 1)
                        for g in (-1, 0, 1, 2):
                            self.transformer(g)
                        with self.eng.Fori(3, GROUPS - 1) as g:
                            self.transformer(g)
                        for g in (GROUPS - 1, GROUPS, GROUPS + 1):
                            self.transformer(g)
                        self.alone(PREP_STEPS, 2, 0)
                        self.ahead(2)
                    self.group(layer, 0)
                    with self.eng.Fori(1, GROUPS - 2) as g:
                        self.group(layer, g)
                    self.group(layer, GROUPS - 2)
                    self.group(layer, GROUPS - 1)
                self.tail(until - 1, GROUPS - 1)

        def follows(layer, g):
            return not (isinstance(g, int) and g == GROUPS - 1 and (layer in (1, 3) or layer == until - 1))

        def job_at(layer, g, job):
            if job < JOBS[layer]:
                return layer, g, job
            if isinstance(g, int) and g == GROUPS - 1:
                return layer + 1, 0, job - JOBS[layer]
            return layer, g + 1, job - JOBS[layer]

        @block.sync
        def _(sp):
            x_in = x.rearrange("b n d -> n b d")
            x_out = out.rearrange("b n d -> n b d")
            XV = X[:, :].rearrange("p (b d) -> p b d", d=P)
            adj_v = adj.rearrange("b i j -> i b j")
            adjT_v = adjT.rearrange("b i j -> i b j")

            def load_adj(layer, g):
                if layer == 3 and isinstance(g, int) and g < 2:
                    sp.wait_ge(t_pen.sem, t_pen.at(2, GROUPS - 1))
                elif layer or not isinstance(g, int) or g >= 2:
                    la, gr = (layer, g - 2) if not (isinstance(g, int) and g < 2) else (layer - 1, GROUPS - 2 + g)
                    sp.wait_ge(g_pen.sem, g_pen.at(la, gr))
                if due(adj_in.before(layer, g)):
                    sp.wait_ge(adj_in.sem, adj_in.before(layer, g))
                if layer == 2:
                    return
                src = adjT_v if layer == 1 else adj_v
                sp.dma_start(graphs(half(ADJ, g)), src[:, span(g * PER_GROUP, PER_GROUP), :])\
                    .then_inc(adj_in.sem, 16)

            sp.dma_start(XV[:, 0:8, :], x_in[:, 0:8, :]).then_inc(x_first, 16)
            load_adj(0, 0)
            load_adj(0, 1)
            sp.dma_start(XV[:, 8:GRAPHS, :], x_in[:, 8:GRAPHS, :]).then_inc(x_rest, 16)
            sp.dma_start(H[:, :], l0_w1).then_inc(stage_in, 16)
            if until > 1:
                sp.dma_start(T[:, 0:768], l1_w1).then_inc(stage_in, 16)
            sp.dma_start(WA_F[:, 0:2048], l0_w2).then_inc(w2_in, 16)
            if until > 1:
                sp.dma_start(WA_F[:, 2048:2816], l1_w2).then_inc(w2_in, 16)
                sp.dma_start(WA_F[:, 2816:3584], l1_w3).then_inc(w2_in, 16)
            if until > 2:
                sp.dma_start(WB_F[:, :], l2_w2).then_inc(w2_in, 16)

            def load_both(g):
                if due(t_pen.before(2, g)):
                    sp.wait_ge(t_pen.sem, t_pen.before(2, g))
                for n, src in enumerate((adj_v, adjT_v)):
                    sp.dma_start(graphs(ADJ[:, n * TOK:(n + 1) * TOK]),
                                 src[:, span(g * PER_GROUP, PER_GROUP), :]).then_inc(adj_in.sem, 16)

            for layer in layers:
                if layer == 2:
                    sp.wait_ge(g_ad.sem, g_ad.at(1, GROUPS - 1))
                    sp.dma_start(SCR[:, 0:4096], l2_w1).then_inc(stage_in, 16)
                    if due(adj_in.before(2, 0)):
                        sp.wait_ge(adj_in.sem, adj_in.before(2, 0))
                    load_both(0)
                    with sp.Fori(1, GROUPS) as g:
                        load_both(g)
                    sp.wait_ge(t_x.sem, t_x.at(2, GROUPS - 1))
                    if until > 3:
                        sp.dma_start(SCR[:, 0:4096], l3_w1).then_inc(stage_in, 16)
                        sp.dma_start(WA_F[:, :], l3_w2).then_inc(w2_in, 16)
                    continue
                if layer:
                    for g in (0, 1):
                        load_adj(layer, g)
                with sp.Fori(1, GROUPS - 1) as g:
                    load_adj(layer, g + 1)
            with sp.Fori(0, GROUPS) as g:
                sp.wait_ge(tail_x.sem, tail_x.at(until - 1, g))
                sp.dma_start(x_out[:, span(g * PER_GROUP, PER_GROUP), :],
                             XV[:, span(g * PER_GROUP, PER_GROUP), :]).then_inc(stored, 16)
            sp.wait_ge(stored, 16 * GROUPS)

        @block.gpsimd
        def _(pool):
            def link(ins, sem_, count=[0]):
                count[0] += 1
                ins.then_inc(sem_, 1)
                pool.wait_ge(sem_, count[0])

            link(pool.memset(IDF[:, :], 0.0), consts)
            link(pool.affine_select(out=IDF[:, :], in_=IDF[:, :], compare_op=ALU.not_equal, fill=1.0,
                                    base=0, pattern=[[-1, P]], channel_multiplier=1), consts)
            link(pool.memset(IDB[:, :], 0.0), consts)
            link(pool.affine_select(out=IDB[:, :], in_=IDB[:, :], compare_op=ALU.not_equal, fill=1.0,
                                    base=0, pattern=[[-1, P]], channel_multiplier=1), consts)
            link(pool.memset(SEL[:, :], 0.0), consts)
            sel = SEL[:, :].rearrange("p (e n) -> p e n", n=P)
            for part in range(3):
                link(pool.affine_select(out=sel, in_=sel, compare_op=ALU.not_equal, fill=1.0,
                                        base=-8 * part, pattern=[[-1, 8], [0, P]], channel_multiplier=1), consts)
            for e in range(8):
                link(pool.memset(IOTA[:, e:e + 1], 64.0 + e), consts)
            link(pool.memset(POW[:, :], -0.5), consts)
            link(pool.memset(NEB[:, :], BARRED), consts)
            link(pool.affine_select(out=NEB[:, :], in_=NEB[:, :], compare_op=ALU.not_equal, fill=0.0,
                                    base=0, pattern=[[-1, P]], channel_multiplier=1), consts)
            link(pool.memset(HM[:, :], 1.0), consts)
            link(pool.affine_select(out=HM[:, :], in_=HM[:, :], compare_op=ALU.is_ge, fill=0.0,
                                    base=0, pattern=[[-HD, HEADS]], channel_multiplier=1), consts)
            link(pool.affine_select(out=HM[:, :], in_=HM[:, :], compare_op=ALU.is_ge, fill=0.0,
                                    base=HD - 1, pattern=[[HD, HEADS]], channel_multiplier=-1), consts)

            def slot(layer, g, e):
                if e > 0:
                    pool.wait_ge(comb.sem, comb.at(layer, g, e + 1))
                    if e > 1:
                        pool.wait_ge(acc_done.sem, acc_done.at(layer, g, e - 1))
                    pool.tensor_tensor(ACC[:, :], ACC[:, :], T[:, (e % 2) * TOK:(e % 2 + 1) * TOK],
                                       ALU.add).then_inc(acc_done.sem, 1)

            def p_apply(layer, g):
                pool.wait_ge(p_ln.sem, p_ln.at(layer, g, 9))
                pool.tensor_tensor(RS[:, :], RS[:, :], POW[:, :], ALU.pow).then_inc(p_rs.sem, 1)

            def p_apply2(layer, g):
                pool.wait_ge(p_ln.sem, p_ln.at(layer, g, 22))
                pool.tensor_tensor(RS[:, :], RS[:, :], POW[:, :], ALU.pow).then_inc(p_rs.sem, 1)

            def g_apply(layer, g):
                pool.wait_ge(g_ln.sem, g_ln.at(layer, g, 9))
                pool.tensor_tensor(GRS[:, :], GRS[:, :], POW[:, :], ALU.pow).then_inc(g_rs.sem, 1)

            def t_pow(g, n):
                source = (t_ln, t_n1, t_x)[n]
                pool.wait_ge(source.sem, source.at(2, g, (9, 11, 10)[n]))
                r = (GRS, RS, RV[:, 12:16])[n]
                pool.tensor_tensor(r[:, 0:4], r[:, 0:4], POW[:, :], ALU.pow).then_inc(t_rw[n].sem, 1)

            def t_keys(g, b):
                pool.wait_ge(t_kt.sem, t_kt.at(2, g))
                if due(t_sc.before(2, g) + b - 1):
                    pool.wait_ge(t_sc.sem, t_sc.before(2, g) + b - 1)
                keys = TKT_RING[:, span((g % 2) * TOK + b * P, P)]
                pool.tensor_tensor(TKM[b % 2].rearrange("p (h n) -> p h n", n=P),
                                   keys.unsqueeze(1).to_broadcast([P, HEADS, P]),
                                   HM[:, :].unsqueeze(2).to_broadcast([P, HEADS, P]), ALU.mult)\
                    .then_inc(t_km.sem, 1)

            Walk(pool, slot, lambda layer, g: None, dict(t_pow=t_pow, t_keys=t_keys, p_apply=p_apply, p_apply2=p_apply2, g_apply=g_apply), lambda: None, lambda layer: None).run()

        N_CONSTS = 22

        @block.tensor
        def _(pe):
            def turn(dst, src):
                for b in range(PER_GROUP):
                    last = pe.transpose(dst[:, b * P:(b + 1) * P], src[:, b * P:(b + 1) * P], IDF[:, :])
                return last

            def up(layer, g, job):
                if not follows(layer, g) and job >= JOBS[layer]:
                    return
                layer, g, job = job_at(layer, g, job)
                if layer == 3 and isinstance(g, int) and g == 0 and job == 0:
                    pe.wait_ge(w_split, 8)
                    pe.wait_ge(w2_in, 16 * 5)
                if job == 0:
                    pe.wait_ge(p_sp.sem, p_sp.at(layer, g))
                if due(h_done.before(layer, g) + job - 1):
                    pe.wait_ge(h_done.sem, h_done.before(layer, g) + job - 1)
                z = Z[job % 2]
                r, at, n = W1[layer]
                if layer == 1 and job not in L1_FIRST:
                    e = L1_SECOND.index(job)
                    pe.wait_ge(h_done.sem, h_done.at(1, g, L1_FIRST[e] + 1))
                    last = pe.matmul(z[:, :], WA_F[:, 2048 + e * P:2048 + (e + 1) * P],
                                     hidden(L1_FIRST[e]), start=True, stop=True)
                else:
                    e = L1_FIRST.index(job) if layer == 1 else job
                    hi = r[:, at + e * P:at + (e + 1) * P]
                    lo = r[:, at + n + e * P:at + n + (e + 1) * P]
                    pe.matmul(z[:, :], lo, half(XH, g), start=True, stop=False)
                    pe.matmul(z[:, :], hi, half(XL, g), start=False, stop=False)
                    last = pe.matmul(z[:, :], hi, half(XH, g), start=False, stop=True)
                last.then_inc(z_full.sem, 1)

            def hidden(job):
                return H[:, (job % HB) * TOK:(job % HB + 1) * TOK]

            def gates_free(layer, g, e):
                if e == 0:
                    pe.wait_ge(p_ge.sem, p_ge.at(layer, g))
                if due(gs_done.before(layer, g) + e):
                    pe.wait_ge(gs_done.sem, gs_done.before(layer, g) + e)

            def gates(layer, g, e):
                pe.matmul(GB[:, :], SEL[:, e * P:(e + 1) * P], half(GT, g, 24), start=True, stop=True)\
                    .then_inc(g_full.sem, 1)

            def slot(layer, g, e):
                if e < 0:
                    up(layer, g, 2)
                    return
                nb = BLOCKS[layer]
                y = Y[e % 2]
                w2, at = W2[layer]
                if due(comb.before(layer, g) + e - 1):
                    pe.wait_ge(comb.sem, comb.before(layer, g) + e - 1)
                if layer == 1:
                    gates_free(layer, g, e)
                    pe.wait_ge(h_done.sem, h_done.at(1, g, L1_SECOND[e] + 1))
                    pe.matmul(y[:, :], WA_F[:, 2816 + e * P:2816 + (e + 1) * P], hidden(L1_SECOND[e]),
                              start=True, stop=True).then_inc(y_full.sem, 1)
                    gates(layer, g, e)
                    up(layer, g, 2 * e + 3)
                    up(layer, g, 2 * e + 4)
                    return
                for k in range(nb):
                    job = e * nb + k
                    if k == 0:
                        gates_free(layer, g, e)
                    pe.wait_ge(h_done.sem, h_done.at(layer, g, job + 1))
                    last = pe.matmul(y[:, :], w2[:, at + job * P:at + (job + 1) * P], hidden(job),
                                     start=(k == 0), stop=(k == nb - 1))
                    if k == nb - 1:
                        last.then_inc(y_full.sem, 1)
                    if k == 0:
                        gates(layer, g, e)
                    up(layer, g, job + 2)

            def tail(layer, g):
                pe.wait_ge(acc_done.sem, acc_done.at(layer, g))
                turn(PC, ACC).then_inc(tail_tr.sem, 1)

            def p_turn(layer, g):
                pe.wait_ge(p_ln.sem, p_ln.at(layer, g, 13))
                if layer != 0 or not (isinstance(g, int) and g == 0):
                    if due(tail_x.before(layer, g) - 1):
                        pe.wait_ge(tail_x.sem, tail_x.before(layer, g) - 1)
                    if due(p_ge.before(layer, g)):
                        pe.wait_ge(p_ge.sem, p_ge.before(layer, g))
                turn(PC, PX).then_inc(p_tr.sem, 1)

            def p_router(layer, g):
                pe.wait_ge(p_ev.sem, p_ev.at(layer, g))
                pe.matmul(PC[0:64, :], mat("l1_rw1"), PT[:, :], start=True, stop=True).then_inc(p_r1.sem, 1)

            def p_logits(layer, g):
                if layer == 1:
                    pe.wait_ge(p_rh.sem, p_rh.at(layer, g))
                    for b in range(PER_GROUP):
                        last = pe.matmul(PC[:, b * 8:b * 8 + 6], PX[0:64, b * P:(b + 1) * P],
                                         mat("l1_rw2")[0:64, :], start=True, stop=True)
                else:
                    pe.wait_ge(p_ev.sem, p_ev.at(layer, g, 1))
                    for b in range(PER_GROUP):
                        last = pe.matmul(PC[:, b * 8:b * 8 + 8], PT[:, b * P:(b + 1) * P],
                                         mat(f"l{layer}_wg"), start=True, stop=True)
                last.then_inc(p_lg.sem, 1)

            def p_gates(layer, g):
                pe.wait_ge(p_dv.sem, p_dv.at(layer, g))
                pe.wait_ge(p_ev.sem, p_ev.at(layer, g))
                gt = PC[:, 0:TOK // 2].bitcast(BF16)
                for b in range(PER_GROUP):
                    last = pe.transpose(gt[0:24, b * P:(b + 1) * P], GB3[:, b * 24:(b + 1) * 24], IDB[:, :])
                last.then_inc(p_gt.sem, 1)

            def g_turn(layer, g):
                pe.wait_ge(g_ln.sem, g_ln.at(layer, g))
                turn(PA, GXN).then_inc(g_tr.sem, 1)

            def g_scores(layer, g):
                pe.wait_ge(g_ev.sem, g_ev.at(layer, g))
                pe.wait_ge(g_pen.sem, g_pen.at(layer, g))
                w = mat("l0_wT") if layer == 0 else mat("l3_w")
                v = 0 if layer == 0 else 2 * P
                for b in range(PER_GROUP):
                    pe.matmul(PB[:, b * P:(b + 1) * P], GXT[:, b * P:(b + 1) * P], w, start=True, stop=True)
                pe.matmul(PA[:, :], V[:, v + P:v + 2 * P], GXT, start=True, stop=False, skip_group_check=True)
                for b in range(PER_GROUP):
                    pe.matmul(PA[:, b * P:(b + 1) * P], GXT[:, b * P:(b + 1) * P], V[:, v:v + P],
                              start=False, stop=False, skip_group_check=True)
                pe.matmul(PA[:, :], IDB[:, :], PEN[:, :], start=False, stop=True, skip_group_check=True)\
                    .then_inc(g_sc.sem, 1)

            def g_turn_p(layer, g):
                pe.wait_ge(g_ex.sem, g_ex.at(layer, g))
                turn(PA, GP).then_inc(g_pt.sem, 1)

            def g_mix(layer, g):
                if layer == 1:
                    pe.wait_ge(g_ev.sem, g_ev.at(layer, g))
                    for b in range(PER_GROUP):
                        for r in range(RELATIONS):
                            at = (b * RELATIONS + r) * P
                            last = pe.matmul(PA[:, b * P:(b + 1) * P], GHT[:, at:at + P],
                                             mat("l1_w", r * P, P), start=(r == 0), stop=(r == RELATIONS - 1))
                else:
                    pe.wait_ge(g_pe.sem, g_pe.at(layer, g))
                    for b in range(PER_GROUP):
                        last = pe.matmul(PB[:, b * P:(b + 1) * P], GPT[:, b * P:(b + 1) * P],
                                         GH[:, b * P:(b + 1) * P], start=True, stop=True)
                last.then_inc(g_mx.sem, 1)

            def relations(layer, g, pair):
                pe.wait_ge(g_ln.sem, g_ln.at(layer, g))
                pe.wait_ge(g_pen.sem, g_pen.at(layer, g))
                if pair:
                    pe.wait_ge(g_ev.sem, g_ev.at(layer, g, 2))
                for b, bank in ((2 * pair, PA), (2 * pair + 1, PB)):
                    last = pe.matmul(bank[:, :], GXN[:, b * P:(b + 1) * P],
                                     GM[:, b * RELATIONS * P:(b + 1) * RELATIONS * P], start=True, stop=True)
                last.then_inc(g_tr.sem, 1)

            def p_turn2(layer, g):
                pe.wait_ge(p_ln.sem, p_ln.at(layer, g))
                pe.wait_ge(p_dv.sem, p_dv.at(layer, g, 1))
                turn(PC, PX2).then_inc(p_tr.sem, 1)

            def w2_bias(layer, g):
                pe.wait_ge(stage_in, 48)
                for e in range(8):
                    for k in range(4):
                        at = (e * 4 + k) * P
                        last = pe.matmul(PA[:, e * 4 + k:e * 4 + k + 1], SCR[:, at:at + P],
                                         col("l2_lnb", e), start=True, stop=True)
                last.then_inc(w_bias, 1)

            def t_turn(g, b):
                pe.wait_ge(t_ln.sem, t_ln.at(2, g))
                if due(t_mh.before(2, g) - 8):
                    pe.wait_ge(t_mh.sem, t_mh.before(2, g) - 8)
                turn(Y[0], TU).then_inc(t_tr.sem, 1)

            def t_project(g, b):
                pe.wait_ge(t_ut.sem, t_ut.at(2, g))
                pe.matmul(Y[0], mat("l2_wk"), TT, start=True, stop=True).then_inc(t_qkv.sem, 1)
                if due(t_mh.before(2, g) - 8):
                    pe.wait_ge(t_mh.sem, t_mh.before(2, g) - 8)
                pe.matmul(Y[1], mat("l2_wq"), TT, start=True, stop=True).then_inc(t_qkv.sem, 1)
                if due(t_n1.before(2, g) - 36 + 1 if not isinstance(g, int) or g >= 2 else 0):
                    pe.wait_ge(t_n1.sem, t_n1.before(2, g) - 36 + 1 if not isinstance(g, int) or g >= 2 else 0)
                for n in range(PER_GROUP):
                    last = pe.matmul(PB[:, n * P:(n + 1) * P], TT[:, n * P:(n + 1) * P], mat("l2_wv"),
                                     start=True, stop=True)
                last.then_inc(t_qkv.sem, 1)

            def t_scores(g, b):
                if b == 0:
                    pe.wait_ge(t_qt.sem, t_qt.at(2, g))
                    pe.wait_ge(t_pen.sem, t_pen.at(2, g))
                pe.wait_ge(t_km.sem, t_km.at(2, g, b + 1))
                if due(t_ce.before(2, g) + 2 * b):
                    pe.wait_ge(t_ce.sem, t_ce.before(2, g) + 2 * b)
                mask = PEN[:, b * P:(b + 1) * P].unsqueeze(1).to_broadcast([P, 4, P])
                for n in range(2):
                    pe.matmul(Z[n].rearrange("p (h n) -> p h n", n=P), IDB[:, :], mask,
                              start=True, stop=False, skip_group_check=True)
                    last = pe.matmul(Z[n], TQT[:, b * P:(b + 1) * P], TKM[b % 2][:, n * TOK:(n + 1) * TOK],
                                     start=False, stop=True, skip_group_check=True)
                last.then_inc(t_sc.sem, 1)

            def t_turn_p(g, b):
                pe.wait_ge(t_ex.sem, t_ex.at(2, g, b + 1))
                if due(t_pe.before(2, g) + b):
                    pe.wait_ge(t_pe.sem, t_pe.before(2, g) + b)
                for h in range(HEADS):
                    last = pe.transpose(QQ[:, h * P:(h + 1) * P], TE[:, h * P:(h + 1) * P], IDF[:, :])
                last.then_inc(t_tp.sem, 1)

            def t_mix(g, b):
                pe.wait_ge(t_pe.sem, t_pe.at(2, g, b + 1))
                if b == 0:
                    pe.wait_ge(t_ve.sem, t_ve.at(2, g))
                if due(t_cx.before(2, g) + 2 * b):
                    pe.wait_ge(t_cx.sem, t_cx.before(2, g) + 2 * b)
                for h in range(HEADS):
                    at = (b % 2) * 256 + h * (HD + 1)
                    last = pe.matmul(PC[:, at:at + HD + 1], TPT[:, h * P:(h + 1) * P],
                                     TVE[:, span((g % 2) * 4 * VE_ROW + b * VE_ROW + h * (HD + 1), HD + 1)],
                                     start=True, stop=True)
                last.then_inc(t_pv.sem, 1)

            def t_turn_c(g, b):
                pe.wait_ge(t_cx.sem, t_cx.at(2, g))
                pe.wait_ge(t_ve.sem, t_ve.at(2, g + 1 if not (isinstance(g, int) and g == GROUPS - 1) else g))
                turn(PB, TC).then_inc(t_ct.sem, 1)

            def t_out(g, b):
                pe.wait_ge(t_cv.sem, t_cv.at(2, g))
                for n in range(PER_GROUP):
                    last = pe.matmul(PB[:, n * P:(n + 1) * P], TT[:, n * P:(n + 1) * P], mat("l2_wo"),
                                     start=True, stop=True)
                last.then_inc(t_wo.sem, 1)

            def t_turn_n(g, b):
                pe.wait_ge(t_n1.sem, t_n1.at(2, g))
                pe.wait_ge(t_qt.sem, t_qt.at(2, g + 2 if not (isinstance(g, int) and g >= GROUPS - 2) else GROUPS - 1))
                turn(Y[1], TN1).then_inc(t_t1.sem, 1)

            def t_mlp1(g, half_):
                pe.wait_ge(t_nt.sem, t_nt.at(2, g))
                if half_ == 0:
                    if due(t_x.before(2, g)):
                        pe.wait_ge(t_x.sem, t_x.before(2, g))
                for k in (2 * half_, 2 * half_ + 1):
                    if half_:
                        pe.wait_ge(t_mh.sem, t_mh.at(2, g, k - 1))
                    pe.matmul(Y[k % 2], mat("l2_w1", k * P, P), TNT, start=True, stop=True)\
                        .then_inc(t_m1.sem, 1)

            def t_mlp2(g, b):
                pe.wait_ge(t_mh.sem, t_mh.at(2, g))
                pe.wait_ge(t_kt.sem, t_kt.at(2, g + 3 if not (isinstance(g, int) and g >= GROUPS - 3) else GROUPS - 1))
                for n in range(PER_GROUP):
                    for k in range(4):
                        last = pe.matmul(Y[0][:, n * P:(n + 1) * P], H[:, k * TOK + n * P:k * TOK + (n + 1) * P],
                                         mat("l2_w2", k * P, P), start=(k == 0), stop=(k == 3))
                last.then_inc(t_m2.sem, 1)

            def begin():
                pe.wait_ge(consts, N_CONSTS)
                pe.wait_ge(small_in, 48)
                for n, (w, a) in enumerate((("l0_w", "l0_a"), ("l3_wT", "l3_a"))):
                    for side in range(2):
                        last = pe.matmul(PA[:, (2 * n + side) * P:(2 * n + side + 1) * P], mat(w),
                                         col(a, side).to_broadcast([P, P]), start=True, stop=True)
                last.then_inc(v_mm, 1)
                pe.wait_ge(v_done, 1)

            def ahead(layer):
                if layer == 0:
                    pe.wait_ge(w2_in, 16 * (1, 3, 4, 4)[until - 1])
                    pe.wait_ge(w_split, 4 if until > 1 else 2)
                else:
                    pe.wait_ge(w_split, 6)
                    pe.wait_ge(t_x.sem, t_x.at(2, GROUPS - 1))
                for job in range(2):
                    up(layer, 0, job)

            Walk(pe, slot, tail, dict(t_turn=t_turn, t_project=t_project, t_scores=t_scores,
                                      t_turn_p=t_turn_p, t_mix=t_mix, t_turn_c=t_turn_c, t_out=t_out,
                                      t_turn_n=t_turn_n, t_mlp1=t_mlp1, t_mlp2=t_mlp2,
                                      p_turn2=p_turn2, w2_bias=w2_bias, p_turn=p_turn, p_router=p_router, p_logits=p_logits,
                                      p_gates=p_gates, g_turn=g_turn, g_scores=g_scores,
                                      g_turn_p=g_turn_p, g_mix=g_mix,
                                      g_rel0=lambda la, g: relations(la, g, 0),
                                      g_rel1=lambda la, g: relations(la, g, 1)), begin, ahead).run()

        @block.scalar
        def _(act):
            def hidden_act(layer, g, job):
                if not follows(layer, g) and job >= JOBS[layer]:
                    return
                layer, g, job = job_at(layer, g, job)
                act.wait_ge(z_full.sem, z_full.at(layer, g, job + 1))
                if layer == 1:
                    bias = col("l1_b1", L1_FIRST.index(job)) if job in L1_FIRST else \
                        col("l1_b2", L1_SECOND.index(job))
                elif layer == 2:
                    bias = LNB1[:, job:job + 1]
                else:
                    bias = col(f"l{layer}_b1", job)
                act.activation(H[:, (job % HB) * TOK:(job % HB + 1) * TOK], Z[job % 2][:, :],
                               ACT.Gelu if layer in (0, 2) else ACT.Relu, bias=bias).then_inc(h_done.sem, 1)

            def slot(layer, g, e):
                if e < 0:
                    hidden_act(layer, g, 2)
                    return
                nb = BLOCKS[layer]

                def gate():
                    act.wait_ge(g_full.sem, g_full.at(layer, g, e + 1))
                    if due(comb.before(layer, g) + e - 1):
                        act.wait_ge(comb.sem, comb.before(layer, g) + e - 1)
                    act.activation(GS[:, (e % 2) * TOK:(e % 2 + 1) * TOK], GB[:, :], ACT.Copy)\
                        .then_inc(gs_done.sem, 1)

                if layer == 1:
                    gate()
                    hidden_act(layer, g, 2 * e + 3)
                    hidden_act(layer, g, 2 * e + 4)
                    return
                for k in range(nb):
                    if k == 0:
                        gate()
                    hidden_act(layer, g, e * nb + k + 2)

            def p_turn(layer, g):
                act.wait_ge(p_tr.sem, p_tr.at(layer, g, 1))
                act.activation(PT[:, :], PC[:, :], ACT.Copy).then_inc(p_ev.sem, 1)

            def p_router(layer, g):
                act.wait_ge(p_r1.sem, p_r1.at(layer, g))
                act.activation(PX[0:64, :], PC[0:64, :], ACT.Relu,
                               bias=COLW[0:64, COL_AT["l1_rb1"][0]:COL_AT["l1_rb1"][0] + 1]).then_inc(p_rh.sem, 1)

            def p_route(layer, g):
                if layer == 1:
                    act.wait_ge(p_dv.sem, p_dv.at(layer, g, ROUTE_1))
                    act.activation(RT[:, EXPS], RT[:, EXPS], ACT.Exp).then_inc(p_ex.sem, 1)
                    act.wait_ge(p_dv.sem, p_dv.at(layer, g, ROUTE_2))
                    act.activation(RV[:, 8:12], RV[:, 8:12], ACT.Exp).then_inc(p_ex.sem, 1)
                elif layer > 1:
                    act.wait_ge(p_dv.sem, p_dv.at(layer, g, ROUTE_3))
                    act.activation(RV[:, 8:12], RV[:, 8:12], ACT.Exp).then_inc(p_ex.sem, 1)

            def p_gates(layer, g):
                act.wait_ge(p_gt.sem, p_gt.at(layer, g))
                act.activation(half(GT, g, 24), PC[0:24, 0:TOK // 2].bitcast(BF16), ACT.Copy)\
                    .then_inc(p_ge.sem, 1)

            def g_turn(layer, g):
                act.wait_ge(g_tr.sem, g_tr.at(layer, g))
                act.activation(GXT, PA[:, :], ACT.Copy).then_inc(g_ev.sem, 1)

            def g_scores(layer, g):
                act.wait_ge(g_sc.sem, g_sc.at(layer, g))
                if layer == 0:
                    act.activation(GZ, PA[:, :], ACT.Copy).then_inc(g_se.sem, 1)
                act.activation(GH, PB[:, :], ACT.Copy).then_inc(g_se.sem, 1)

            def g_exp(layer, g):
                act.wait_ge(g_ce.sem, g_ce.at(layer, g))
                act.activation(GP, GE, ACT.Exp).then_inc(g_ex.sem, 1)

            def g_turn_p(layer, g):
                act.wait_ge(g_pt.sem, g_pt.at(layer, g))
                act.activation(GPT, PA[:, :], ACT.Copy).then_inc(g_pe.sem, 1)

            def relations(layer, g, pair):
                act.wait_ge(g_tr.sem, g_tr.at(layer, g, pair + 1))
                for b, bank in ((2 * pair, PA), (2 * pair + 1, PB)):
                    act.activation(GHT[:, b * RELATIONS * P:(b + 1) * RELATIONS * P], bank[:, :], ACT.Copy)\
                        .then_inc(g_ev.sem, 1)

            def g_add(layer, g):
                if layer == 3:
                    act.wait_ge(g_ad.sem, g_ad.at(layer, g, 2))
                    act.activation(GE, GZ, ACT.Exp).then_inc(g_el.sem, 1)

            def p_turn2(layer, g):
                act.wait_ge(p_tr.sem, p_tr.at(layer, g, 2))
                act.wait_ge(p_lg.sem, p_lg.at(layer, g))
                act.activation(PT[:, :], PC[:, :], ACT.Copy).then_inc(p_ev.sem, 1)

            def t_turn(g, b):
                act.wait_ge(t_tr.sem, t_tr.at(2, g))
                act.activation(TT, Y[0], ACT.Copy).then_inc(t_ut.sem, 1)

            def t_project(g, b):
                act.wait_ge(t_qkv.sem, t_qkv.at(2, g, 1))
                act.activation(TKT_RING[:, span((g % 2) * TOK, TOK)], Y[0], ACT.Identity,
                               bias=col("l2_bk")).then_inc(t_kt.sem, 1)

            def t_queries(g, b):
                act.wait_ge(t_qkv.sem, t_qkv.at(2, g, 2))
                if due(t_sc.before(2, g)):
                    act.wait_ge(t_sc.sem, t_sc.before(2, g))
                act.activation(TQT, Y[1], ACT.Identity, bias=BQ4[:, :], scale=HD ** -0.5)\
                    .then_inc(t_qt.sem, 1)

            def t_scores(g, b):
                act.wait_ge(t_ce.sem, t_ce.at(2, g, 2 * b + 2))
                act.activation(TE, TE, ACT.Exp).then_inc(t_ex.sem, 1)

            def t_turn_p(g, b):
                act.wait_ge(t_tp.sem, t_tp.at(2, g, b + 1))
                act.activation(TPT, QQ[:, :], ACT.Copy).then_inc(t_pe.sem, 1)

            def t_turn_c(g, b):
                act.wait_ge(t_ct.sem, t_ct.at(2, g))
                act.activation(TT, PB[:, :], ACT.Copy).then_inc(t_cv.sem, 1)

            def t_turn_n(g, b):
                act.wait_ge(t_t1.sem, t_t1.at(2, g))
                act.activation(TNT, Y[1], ACT.Copy).then_inc(t_nt.sem, 1)

            def t_mlp1(g, half_):
                for k in (2 * half_, 2 * half_ + 1):
                    act.wait_ge(t_m1.sem, t_m1.at(2, g, k + 1))
                    act.activation(H[:, k * TOK:(k + 1) * TOK], Y[k % 2], ACT.Relu,
                                   bias=col("l2_mb1", k)).then_inc(t_mh.sem, 1)

            def begin():
                act.dma_start(MATW[:, :], mats).then_inc(small_in, 16)
                act.dma_start(COLW[:, :], cols).then_inc(small_in, 16)
                act.dma_start(ROWW[:, :], rows.partition_broadcast(P)).then_inc(small_in, 16)
                act.wait_ge(v_mm, 1)
                act.activation(V[:, :], PA[:, :], ACT.Copy).then_inc(v_done, 1)
                act.wait_ge(consts, N_CONSTS)

            def ahead(layer):
                for job in range(2):
                    hidden_act(layer, 0, job)

            Walk(act, slot, lambda layer, g: None,
                 dict(t_turn=t_turn, t_project=t_project, t_queries=t_queries, t_scores=t_scores,
                      t_turn_p=t_turn_p, t_turn_c=t_turn_c, t_turn_n=t_turn_n, t_mlp1=t_mlp1,
                      p_turn2=p_turn2, p_turn=p_turn, p_router=p_router, p_route=p_route, p_gates=p_gates, g_turn=g_turn,
                      g_scores=g_scores, g_exp=g_exp, g_turn_p=g_turn_p, g_add=g_add,
                      g_rel0=lambda la, g: relations(la, g, 0),
                      g_rel1=lambda la, g: relations(la, g, 1)), begin, ahead).run()

        @block.vector
        def _(dve):
            def norm_stats(ch, src, st, mv, rs):
                for b in range(PER_GROUP):
                    dve.bn_stats(st[:, 6 * b:6 * b + 6], src(b)).then_inc(ch.sem, ch.one())
                dve.wait_ge(ch.sem, ch.value())
                dve.memset(rs[:, :], EPS)
                for b in range(PER_GROUP):
                    dve.bn_aggr(mv[:, 2 * b:2 * b + 2], st[:, 6 * b:6 * b + 6]).then_inc(ch.sem, ch.one())
                dve.wait_ge(ch.sem, ch.value())
                var = graphs(mv[:, :], 2)[:, :, 1]
                dve.tensor_tensor(rs[:, :], var, rs[:, :], ALU.add).then_inc(ch.sem, ch.one())

            def norm_apply(ch, src, dst, mv, rs):
                for b in range(PER_GROUP):
                    dve.tensor_scalar(dst[:, b * P:(b + 1) * P], src(b), mv[:, 2 * b:2 * b + 1],
                                             rs[:, b:b + 1], ALU.subtract, ALU.mult).then_inc(ch.sem, ch.one())
                dve.wait_ge(ch.sem, ch.value())

            def x_graph(g):
                return lambda b: X[:, span(g * TOK + b * P, P)]

            def slot(layer, g, e):
                if e < 0:
                    return
                dve.wait_ge(y_full.sem, y_full.at(layer, g, e + 1))
                dve.wait_ge(gs_done.sem, gs_done.at(layer, g, e + 1))
                if e == 0:
                    if layer or not (isinstance(g, int) and g == 0):
                        if due(tail_tr.before(layer, g)):
                            dve.wait_ge(tail_tr.sem, tail_tr.before(layer, g))
                    dst = ACC[:, :]
                else:
                    if due(acc_done.before(layer, g) + max(e - 2, 0)):
                        dve.wait_ge(acc_done.sem, acc_done.before(layer, g) + max(e - 2, 0))
                    dst = T[:, (e % 2) * TOK:(e % 2 + 1) * TOK]
                b2 = col("l1_b3" if layer == 1 else f"l{layer}_b2", e)
                dve.scalar_tensor_tensor(dst, Y[e % 2][:, :], b2, GS[:, (e % 2) * TOK:(e % 2 + 1) * TOK],
                                         ALU.add, ALU.mult).then_inc(comb.sem, 1)

            def tail(layer, g):
                dve.wait_ge(tail_tr.sem, tail_tr.at(layer, g))
                dve.tensor_tensor(x_at(g), PC[:, :], x_at(g), ALU.add).then_inc(tail_x.sem, 1)

            def p_norm(layer, g):
                if layer == 2:
                    dve.wait_ge(t_x.sem, t_x.at(layer, g))
                else:
                    dve.wait_ge(g_ad.sem, g_ad.at(layer, g))
                if due(p_lg.before(layer, g)):
                    dve.wait_ge(p_lg.sem, p_lg.before(layer, g))
                norm_stats(Count(p_ln, layer, g), x_graph(g), ST, MV, RS)

            def p_apply(layer, g):
                dve.wait_ge(p_rs.sem, p_rs.at(layer, g, 1))
                norm_apply(Count(p_ln, layer, g, 9), x_graph(g), PX, MV, RS)

            def p_norm2(layer, g):
                norm_stats(Count(p_ln, layer, g, 13), px_graph, ST, MV, RS)

            def p_apply2(layer, g):
                dve.wait_ge(p_rs.sem, p_rs.at(layer, g, 2))
                norm_apply(Count(p_ln, layer, g, 22), px_graph, PX2, MV, RS)

            def px_graph(b):
                return PX[:, b * P:(b + 1) * P]

            def p_split(layer, g):
                dve.wait_ge(p_ev.sem, p_ev.at(layer, g))
                ch = Count(p_sp, layer, g)
                dve.tensor_copy(half(XH, g), PT[:, :]).then_inc(p_sp.sem, ch.one())
                dve.wait_ge(p_sp.sem, ch.value())
                dve.tensor_tensor(half(XL, g), PT[:, :], half(XH, g).bitcast(F32), ALU.subtract).then_inc(p_sp.sem, ch.one())
                ch.full()

            def rt(i):
                return RT[:, 32 * i:32 * i + 32].rearrange("p (b e) -> p b e", e=8)

            def rv(i):
                return RV[:, 4 * i:4 * i + 4]

            def wide(v):
                return v.unsqueeze(2).to_broadcast([P, PER_GROUP, 8])

            def p_route(layer, g):
                dve.wait_ge(p_lg.sem, p_lg.at(layer, g))
                ch = Count(p_dv, layer, g)
                n = EXPERTS[layer]
                iota = IOTA[:, :].unsqueeze(1).to_broadcast([P, PER_GROUP, 8])
                lg, eq, key, one, two, rest, gate = (rt(i) for i in range(7))
                m1, m2, ex, at, w1, w2, t1 = rv(0), rv(1), rv(2), rv(3), rv(4), rv(5), rv(6)
                if layer == 1:
                    dve.memset(lg[:, :, n:8], BARRED).then_inc(p_dv.sem, ch.one())
                dve.tensor_tensor(lg[:, :, 0:n], graphs(PC[:, 0:32], 8)[:, :, 0:n],
                                          row(f"l{layer}_bg").unsqueeze(1).to_broadcast([P, PER_GROUP, n]),
                                          ALU.add).then_inc(p_dv.sem, ch.one())
                dve.wait_ge(p_dv.sem, ch.value())
                for src, m, hot in ((lg, m1, one), (rest, m2, two)):
                    dve.tensor_reduce(m, src, AX, ALU.max).then_inc(p_dv.sem, ch.one())
                    dve.wait_ge(p_dv.sem, ch.value())
                    dve.tensor_tensor(eq, src, wide(m), ALU.is_equal).then_inc(p_dv.sem, ch.one())
                    dve.wait_ge(p_dv.sem, ch.value())
                    dve.scalar_tensor_tensor(key, eq, -64.0, iota, ALU.mult, ALU.add).then_inc(p_dv.sem, ch.one())
                    dve.wait_ge(p_dv.sem, ch.value())
                    dve.tensor_reduce(at, key, AX, ALU.min).then_inc(p_dv.sem, ch.one())
                    dve.wait_ge(p_dv.sem, ch.value())
                    dve.tensor_tensor(hot, key, wide(at), ALU.is_equal).then_inc(p_dv.sem, ch.one())
                    dve.wait_ge(p_dv.sem, ch.value())
                    if hot is one:
                        dve.scalar_tensor_tensor(rest, one, 2 * BARRED, lg, ALU.mult, ALU.add).then_inc(p_dv.sem, ch.one())
                        dve.wait_ge(p_dv.sem, ch.value())
                if layer == 0:
                    dve.tensor_tensor(gate, one, two, ALU.add).then_inc(p_dv.sem, ch.one())
                    dve.wait_ge(p_dv.sem, ch.value())
                else:
                    if layer == 1:
                        e9 = RT[:, EXPS]
                        lgx = e9[:, 0:32].rearrange("p (b e) -> p b e", e=8)
                        dve.tensor_tensor(lgx, lg, wide(m1), ALU.subtract).then_inc(p_dv.sem, ch.one())
                        dve.tensor_tensor(e9[:, 32:36], m2, m1, ALU.subtract).then_inc(p_dv.sem, ch.one())
                        dve.wait_ge(p_dv.sem, ch.value())
                        assert ch.n == ROUTE_1, ch.n
                        dve.wait_ge(p_ex.sem, p_ex.at(layer, g, 1))
                        dve.tensor_reduce(t1, lgx, AX, ALU.add).then_inc(p_dv.sem, ch.one())
                        dve.wait_ge(p_dv.sem, ch.value())
                        dve.reciprocal(t1, t1).then_inc(p_dv.sem, ch.one())
                        dve.wait_ge(p_dv.sem, ch.value())
                        dve.scalar_tensor_tensor(ex, e9[:, 32:36], -1.0, t1, ALU.add, ALU.mult).then_inc(p_dv.sem, ch.one())
                        dve.wait_ge(p_dv.sem, ch.value())
                        assert ch.n == ROUTE_2, ch.n
                        dve.wait_ge(p_ex.sem, p_ex.at(layer, g, 2))
                    else:
                        dve.tensor_tensor(ex, m2, m1, ALU.subtract).then_inc(p_dv.sem, ch.one())
                        dve.wait_ge(p_dv.sem, ch.value())
                        assert ch.n == ROUTE_3, ch.n
                        dve.wait_ge(p_ex.sem, p_ex.at(layer, g))
                    dve.tensor_scalar(w1, ex, 1.0, None, ALU.add).then_inc(p_dv.sem, ch.one())
                    dve.wait_ge(p_dv.sem, ch.value())
                    dve.reciprocal(w1, w1).then_inc(p_dv.sem, ch.one())
                    dve.wait_ge(p_dv.sem, ch.value())
                    dve.tensor_tensor(w2, ex, w1, ALU.mult).then_inc(p_dv.sem, ch.one())
                    dve.wait_ge(p_dv.sem, ch.value())
                    dve.tensor_tensor(one, one, wide(w1), ALU.mult).then_inc(p_dv.sem, ch.one())
                    dve.tensor_tensor(two, two, wide(w2), ALU.mult).then_inc(p_dv.sem, ch.one())
                    dve.wait_ge(p_dv.sem, ch.value())
                    dve.tensor_tensor(gate, one, two, ALU.add).then_inc(p_dv.sem, ch.one())
                    dve.wait_ge(p_dv.sem, ch.value())
                g3 = graphs(GB3[:, :], 24)
                dve.tensor_copy(g3[:, :, 0:8], gate).then_inc(p_dv.sem, ch.one())
                dve.wait_ge(p_dv.sem, ch.value())
                dve.tensor_tensor(gate, gate, g3[:, :, 0:8], ALU.subtract).then_inc(p_dv.sem, ch.one())
                dve.wait_ge(p_dv.sem, ch.value())
                dve.tensor_copy(g3[:, :, 8:16], gate).then_inc(p_dv.sem, ch.one())
                dve.wait_ge(p_dv.sem, ch.value())
                dve.tensor_tensor(g3[:, :, 16:24], gate, g3[:, :, 8:16], ALU.subtract).then_inc(p_dv.sem, ch.one())
                dve.wait_ge(p_dv.sem, ch.value())
                ch.full()

            def g_norm(layer, g):
                if layer == 0 and isinstance(g, int) and g == 2:
                    dve.wait_ge(x_rest, 16)
                if layer:
                    dve.wait_ge(tail_x.sem, tail_x.at(layer - 1, g))
                norm_stats(Count(g_ln, layer, g), x_graph(g), GST, GMV, GRS)
                dve.wait_ge(adj_in.sem, adj_in.at(layer, g))
                pen = Count(g_pen, layer, g)
                a = half(ADJ, g)
                if layer == 1:
                    gm = GM.rearrange("p (b r n) -> p b r n", r=RELATIONS, n=P)
                    for r in range(RELATIONS):
                        dve.tensor_scalar(gm[:, :, r, :], graphs(a), float(r + 1), None, ALU.is_equal).then_inc(g_pen.sem, pen.one())
                else:
                    dve.tensor_scalar(PEN[:, :], a, 0.0, MASKED,
                                              ALU.is_equal if layer == 0 else ALU.is_le, ALU.mult).then_inc(g_pen.sem, pen.one())
                pen.full()

            def g_apply(layer, g):
                dve.wait_ge(g_rs.sem, g_rs.at(layer, g))
                norm_apply(Count(g_ln, layer, g, 9), x_graph(g), GXN, GMV, GRS)

            def g_center(layer, g):
                dve.wait_ge(g_se.sem, g_se.at(layer, g))
                ch = Count(g_ce, layer, g)
                mx = GR[:, 0:4]
                if layer == 0:
                    dve.scalar_tensor_tensor(GE, GZ, 0.2, PA[:, :], ALU.mult, ALU.max).then_inc(g_ce.sem, ch.one())
                    dve.wait_ge(g_ce.sem, ch.value())
                    z = GE
                else:
                    z = PA[:, :]
                dve.tensor_reduce(mx, graphs(z), AX, ALU.max).then_inc(g_ce.sem, ch.one())
                dve.wait_ge(g_ce.sem, ch.value())
                dve.tensor_tensor(graphs(GE), graphs(z), mx.unsqueeze(2).to_broadcast([P, PER_GROUP, P]),
                                         ALU.subtract).then_inc(g_ce.sem, ch.one())
                ch.full()

            def g_turn_p(layer, g):
                dve.wait_ge(g_ex.sem, g_ex.at(layer, g))
                ch = Count(g_su, layer, g)
                dve.tensor_reduce(GR[:, 4:8], graphs(GP), AX, ALU.add).then_inc(g_su.sem, ch.one())
                dve.wait_ge(g_su.sem, ch.value())
                dve.reciprocal(GR[:, 8:12], GR[:, 4:8]).then_inc(g_su.sem, ch.one())
                dve.wait_ge(g_su.sem, ch.value())
                ch.full()

            def g_add(layer, g):
                dve.wait_ge(g_mx.sem, g_mx.at(layer, g))
                ch = Count(g_ad, layer, g)
                if layer == 1:
                    bias = row("l1_bias").unsqueeze(1).to_broadcast([P, PER_GROUP, P])
                    dve.tensor_tensor(graphs(GXN), graphs(PA[:, :]), bias, ALU.add).then_inc(g_ad.sem, ch.one())
                    dve.wait_ge(g_ad.sem, ch.value())
                    dve.tensor_tensor(x_at(g), GXN, x_at(g), ALU.add).then_inc(g_ad.sem, ch.one())
                else:
                    norm_ = GR[:, 8:12].unsqueeze(2).to_broadcast([P, PER_GROUP, P])
                    dve.tensor_tensor(graphs(GP), graphs(PB[:, :]), norm_, ALU.mult).then_inc(g_ad.sem, ch.one())
                    dve.wait_ge(g_ad.sem, ch.value())
                    if layer == 0:
                        dve.tensor_tensor(x_at(g), GP, x_at(g), ALU.add).then_inc(g_ad.sem, ch.one())
                    else:
                        dve.tensor_scalar(GZ, GP, 0.0, None, ALU.min).then_inc(g_ad.sem, ch.one())
                        dve.wait_ge(g_el.sem, g_el.at(layer, g))
                        dve.scalar_tensor_tensor(GP, GP, 0.0, GE, ALU.max, ALU.add).then_inc(g_ad.sem, ch.one())
                        dve.wait_ge(g_ad.sem, ch.value())
                        dve.scalar_tensor_tensor(x_at(g), GP, -1.0, x_at(g), ALU.add, ALU.add).then_inc(g_ad.sem, ch.one())
                ch.full()

            def w2_split(layer, part):
                if part == 0:
                    dve.wait_ge(w_bias, 1)
                    dve.tensor_tensor(LNB1[:, :], PA[:, 0:32], COLW[:, COL_AT["l2_b1"][0]:COL_AT["l2_b1"][0] + 32],
                                      ALU.add).then_inc(l2_consts, 1)
                    dve.tensor_scalar(BQ4[:, :], col("l2_bq"), HD ** -0.5, None, ALU.mult).then_inc(l2_consts, 1)
                    for e in range(8):
                        w = SCR[:, e * 4 * P:(e + 1) * 4 * P]
                        dve.tensor_scalar(w, w, col("l2_lng", e), None, ALU.mult).then_inc(l2_consts, 1)
                elif part == 1:
                    dve.wait_ge(l2_consts, 10)
                    split_weights(SCR[:, 0:4096], 2, 4)

            def w3_split(layer, part):
                if part == 0:
                    dve.wait_ge(stage_in, 64)
                    split_weights(SCR[:, 0:4096], 3, 6)

            def t_norm(g, b):
                dve.wait_ge(tail_x.sem, tail_x.at(1, g))
                if isinstance(g, int) and g == 0:
                    dve.wait_ge(w_split, 6)
                    ones = TVE.rearrange("p (h n) -> p h n", n=HD + 1)[:, :, HD:HD + 1]
                    dve.memset(ones, 1.0).then_inc(l2_consts, 1)
                norm_stats(Count(t_ln, 2, g), x_graph(g), GST, GMV, GRS)

            def t_apply(g, b):
                dve.wait_ge(t_rw[0].sem, t_rw[0].at(2, g))
                norm_apply(Count(t_ln, 2, g, 9), x_graph(g), TU, GMV, GRS)
                ch = Count(t_ln, 2, g, 13)
                dve.tensor_copy(TU_RING[:, span((g % 4) * TOK, TOK)], TU).then_inc(t_ln.sem, ch.one())
                ch.full()

            def t_mask(g, b):
                dve.wait_ge(t_qkv.sem, t_qkv.at(2, g))
                ve = TVE[:, span((g % 2) * 4 * VE_ROW, 4 * VE_ROW)].rearrange("p (b h n) -> p b h n", b=4, n=HD + 1)
                dve.tensor_tensor(ve[:, :, :, 0:HD], PB[:, :].rearrange("p (b h n) -> p b h n", b=4, n=HD),
                                  row("l2_bv").rearrange("p (h n) -> p h n", n=HD).unsqueeze(1)
                                  .to_broadcast([P, 4, HEADS, HD]), ALU.add).then_inc(t_ve.sem, 1)
                dve.wait_ge(adj_in.sem, adj_in.at(2, g))
                if due(t_sc.before(2, g)):
                    dve.wait_ge(t_sc.sem, t_sc.before(2, g))
                ch = Count(t_pen, 2, g)
                dve.tensor_tensor(TM, ADJ[:, 0:TOK], ADJ[:, TOK:2 * TOK], ALU.max).then_inc(t_pen.sem, ch.one())
                dve.wait_ge(t_pen.sem, ch.value())
                dve.scalar_tensor_tensor(graphs(PEN[:, :]), graphs(TM), 0.0,
                                                NEB[:, :].unsqueeze(1).to_broadcast([P, PER_GROUP, P]),
                                                ALU.is_le, ALU.mult).then_inc(t_pen.sem, ch.one())
                ch.full()

            def t_scores(g, b):
                dve.wait_ge(t_sc.sem, t_sc.at(2, g, b + 1))
                ch = Count(t_ce, 2, g, 2 * b)
                s = ZZ[:, :].rearrange("p (h n) -> p h n", n=P)
                mx = RV[:, 16:24]
                dve.tensor_reduce(mx, s, AX, ALU.max).then_inc(t_ce.sem, ch.one())
                dve.wait_ge(t_ce.sem, ch.value())
                dve.tensor_tensor(TE.rearrange("p (h n) -> p h n", n=P), s,
                                         mx.unsqueeze(2).to_broadcast([P, HEADS, P]), ALU.subtract).then_inc(t_ce.sem, ch.one())

            def t_mix(g, b):
                dve.wait_ge(t_pv.sem, t_pv.at(2, g, b + 1))
                ch = Count(t_cx, 2, g, 2 * b)
                o = PC[:, (b % 2) * 256:(b % 2) * 256 + VE_ROW].rearrange("p (h n) -> p h n", n=HD + 1)
                dve.reciprocal(TRC.unsqueeze(2), o[:, :, HD:HD + 1]).then_inc(t_cx.sem, ch.one())
                dve.wait_ge(t_cx.sem, ch.value())
                dve.tensor_tensor(TC[:, b * P:(b + 1) * P].rearrange("p (h n) -> p h n", n=HD),
                                         o[:, :, 0:HD], TRC.unsqueeze(2).to_broadcast([P, HEADS, HD]), ALU.mult).then_inc(t_cx.sem, ch.one())

            def spread(name):
                return row(name).unsqueeze(1).to_broadcast([P, PER_GROUP, P])

            def in_graph(t):
                return lambda b: t[:, b * P:(b + 1) * P]

            def t_out(g, b):
                dve.wait_ge(t_wo.sem, t_wo.at(2, g))
                ch = Count(t_n1, 2, g)
                dve.tensor_tensor(graphs(TN1), graphs(PB[:, :]), spread("l2_bo"), ALU.add).then_inc(t_n1.sem, ch.one())
                dve.wait_ge(t_n1.sem, ch.value())
                dve.tensor_tensor(TN1, TN1, TU_RING[:, span((g % 4) * TOK, TOK)], ALU.add).then_inc(t_n1.sem, ch.one())
                dve.wait_ge(t_n1.sem, ch.value())
                norm_stats(ch, in_graph(TN1), ST, MV, RS)

            def t_norm1(g, b):
                dve.wait_ge(t_rw[1].sem, t_rw[1].at(2, g))
                ch = Count(t_n1, 2, g, 11)
                norm_apply(ch, in_graph(TN1), TN1, MV, RS)
                dve.tensor_tensor(graphs(TN1), graphs(TN1), spread("l2_g1"), ALU.mult).then_inc(t_n1.sem, ch.one())
                dve.wait_ge(t_n1.sem, ch.value())
                dve.tensor_tensor(graphs(TN1), graphs(TN1), spread("l2_c1"), ALU.add).then_inc(t_n1.sem, ch.one())
                dve.wait_ge(t_n1.sem, ch.value())
                dve.tensor_tensor(graphs(TNB_RING[:, span((g % 2) * TOK, TOK)]), graphs(TN1),
                                         spread("l2_mb2"), ALU.add).then_inc(t_n1.sem, ch.one())
                ch.full()

            def t_mlp2(g, b):
                dve.wait_ge(t_m2.sem, t_m2.at(2, g))
                ch = Count(t_x, 2, g)
                dve.tensor_tensor(TR2, Y[0], TNB_RING[:, span((g % 2) * TOK, TOK)], ALU.add).then_inc(t_x.sem, ch.one())
                dve.wait_ge(t_x.sem, ch.value())
                norm_stats(ch, in_graph(TR2), ST2, MV2, RV[:, 12:16])

            def t_norm2(g, b):
                dve.wait_ge(t_rw[2].sem, t_rw[2].at(2, g))
                ch = Count(t_x, 2, g, 10)
                norm_apply(ch, in_graph(TR2), TR2, MV2, RV[:, 12:16])
                dve.tensor_tensor(graphs(TR2), graphs(TR2), spread("l2_g2"), ALU.mult).then_inc(t_x.sem, ch.one())
                dve.wait_ge(t_x.sem, ch.value())
                dve.tensor_tensor(graphs(TR2), graphs(TR2), spread("l2_c2"), ALU.add).then_inc(t_x.sem, ch.one())
                dve.wait_ge(t_x.sem, ch.value())
                dve.tensor_tensor(x_at(g), TR2, x_at(g), ALU.add).then_inc(t_x.sem, ch.one())
                dve.wait_ge(t_x.sem, ch.value())
                ch.full()

            def split_weights(stage, layer, count):
                r, at, n = W1[layer]
                hi, lo = r[:, at:at + n], r[:, at + n:at + 2 * n]
                dve.tensor_copy(hi, stage).then_inc(w_split, 1)
                dve.wait_ge(w_split, count + 1)
                dve.tensor_tensor(lo, stage, hi.bitcast(F32), ALU.subtract).then_inc(w_split, 1)

            def begin():
                dve.wait_ge(x_first, 16)
                dve.wait_ge(consts, N_CONSTS)
                dve.wait_ge(small_in, 48)

            def ahead(layer):
                if layer:
                    return
                dve.wait_ge(stage_in, 32 if until > 1 else 16)
                split_weights(H[:, :], 0, 0)
                if until > 1:
                    split_weights(T[:, 0:768], 1, 2)

            Walk(dve, slot, tail, dict(w2_split=w2_split, w3_split=w3_split, t_norm=t_norm, t_apply=t_apply,
                                       t_mask=t_mask, t_scores=t_scores, t_mix=t_mix, t_out=t_out,
                                       t_norm1=t_norm1, t_mlp2=t_mlp2, t_norm2=t_norm2,
                                       p_norm=p_norm, p_apply=p_apply, p_norm2=p_norm2, p_apply2=p_apply2,
                                       g_apply=g_apply, p_split=p_split, p_route=p_route, g_norm=g_norm,
                                       g_center=g_center, g_turn_p=g_turn_p, g_add=g_add),
                 begin, ahead).run()


def arrange(inputs):
    a = {k: np.asarray(v) for k, v in inputs.items()}

    def column(v, rows=P):
        m = np.zeros((P, v.size // rows), np.float32)
        m[:rows] = v.reshape(-1, rows).T
        return m

    def tall(w):
        e, k, n = w.shape
        return np.ascontiguousarray(w.reshape(e, k // P, P, n).transpose(2, 0, 1, 3).reshape(P, -1))

    def rows64(w):
        m = np.zeros((P, w.shape[1]), np.float32)
        m[:w.shape[0]] = w
        return m

    wqkv, bqkv = a["L2_gnn_Wqkv"], a["L2_gnn_bqkv"]
    cols = dict(
        l0_b1=column(a["L0_ffn_b1"]), l0_b2=column(a["L0_ffn_b2"]), l0_a=column(a["L0_gnn_a"]),
        l1_rb1=column(a["L1_ffn_router_b1"], 64), l1_b1=column(a["L1_ffn_expert_b1"]),
        l1_b2=column(a["L1_ffn_expert_b2"]), l1_b3=column(a["L1_ffn_expert_b3"]),
        l2_bq=column(bqkv[0:P]), l2_bk=column(bqkv[P:2 * P]), l2_mb1=column(a["L2_gnn_b1"]),
        l2_b1=column(a["L2_ffn_b1"]), l2_b2=column(a["L2_ffn_b2"]), l2_lng=column(a["L2_ffn_ln_g"]),
        l2_lnb=column(a["L2_ffn_ln_b"]), l3_a=column(a["L3_gnn_a"]), l3_b1=column(a["L3_ffn_b1"]),
        l3_b2=column(a["L3_ffn_b2"]))
    rows = dict(
        l0_bg=a["L0_ffn_bg"], l1_bg=a["L1_ffn_router_b2"], l2_bg=a["L2_ffn_br"], l3_bg=a["L3_ffn_bg"],
        l1_bias=a["L1_gnn_bias"], l2_bv=bqkv[2 * P:], l2_bo=a["L2_gnn_bo"], l2_g1=a["L2_gnn_ln1_g"],
        l2_c1=a["L2_gnn_ln1_b"], l2_mb2=a["L2_gnn_b2"], l2_g2=a["L2_gnn_ln2_g"], l2_c2=a["L2_gnn_ln2_b"])
    mats = dict(
        l0_wT=a["L0_gnn_W"].T, l0_w=a["L0_gnn_W"], l0_wg=a["L0_ffn_Wg"],
        l1_w=tall(a["L1_gnn_weight"]), l1_rw1=a["L1_ffn_router_w1"], l1_rw2=rows64(a["L1_ffn_router_w2"]),
        l2_wq=wqkv[0:P].T, l2_wk=wqkv[P:2 * P].T, l2_wv=wqkv[2 * P:].T, l2_wo=a["L2_gnn_Wo"].T,
        l2_w1=a["L2_gnn_W1"].T, l2_w2=tall(a["L2_gnn_W2"].T[None]), l2_wg=a["L2_ffn_Wr"],
        l3_w=a["L3_gnn_W"], l3_wT=a["L3_gnn_W"].T, l3_wg=a["L3_ffn_Wg"].T)

    def pack(table, parts):
        for name, n in table:
            assert parts[name].shape[-1] == n, (name, parts[name].shape)
        return np.ascontiguousarray(np.concatenate([parts[name] for name, _ in table], axis=-1))

    return dict(
        x=a["x"], adj=a["adj"], adjT=np.ascontiguousarray(a["adj"].transpose(0, 2, 1)),
        mats=pack(MATS, mats), cols=pack(COLS, cols), rows=pack(ROWS, rows)[None],
        l0_w1=tall(a["L0_ffn_W1"]), l0_w2=tall(a["L0_ffn_W2"]),
        l1_w1=tall(a["L1_ffn_expert_w1"]), l1_w2=tall(a["L1_ffn_expert_w2"]),
        l1_w3=tall(a["L1_ffn_expert_w3"]),
        l2_w1=tall(a["L2_ffn_W1"]), l2_w2=tall(a["L2_ffn_W2"]),
        l3_w1=tall(a["L3_ffn_W1"].transpose(0, 2, 1)), l3_w2=tall(a["L3_ffn_W2"].transpose(0, 2, 1)))


def kernel(**inputs):
    import concourse.bacc as bacc
    from concourse.bass_utils import run_bass_kernel_spmd

    nc = bacc.Bacc("TRN2", target_bir_lowering=False, num_devices=1)
    arrays = arrange(inputs)
    args = [nc.dram_tensor(n, v.shape, mybir.dt.from_np(v.dtype), kind="ExternalInput").ap()
            for n, v in arrays.items()]
    args.append(nc.dram_tensor("out", (GRAPHS, P, P), F32, kind="ExternalOutput").ap())
    build(nc, *args)
    result = run_bass_kernel_spmd(nc, [arrays], core_ids=[0])
    return result.results[0]["out"]
```

```python
from contextlib import ExitStack

import numpy as np
import concourse.bass as bass
from concourse import mybir

F32 = mybir.dt.float32
F32R = mybir.dt.float32r
BF16 = mybir.dt.bfloat16
I32 = mybir.dt.int32
ALU = mybir.AluOpType
ACT = mybir.ActivationFunctionType
AX = mybir.AxisListType.X

P = 128
GRAPHS = 64
PER_GROUP = 4
GROUPS = GRAPHS // PER_GROUP
TOK = PER_GROUP * P
LAYERS = 4
EXPERTS = [8, 6, 8, 8]
BLOCKS = [2, 1, 4, 4]
JOBS = [16, 12, 32, 32]
SLOTS = EXPERTS
HB = 4
AHEAD = [2, 2, 3, 3]
EPS = 1e-5
L1_FIRST = [0, 1, 4, 6, 8, 10]
L1_SECOND = [2, 3, 5, 7, 9, 11]
EXPS = slice(256, 292)
ROUTED = [12, 15, 13, 13]
WEIGHED = 18
MASKED = -float(2 ** 60)
BARRED = -float(2 ** 100)
RELATIONS = 4
HEADS = 8
HD = P // HEADS


class Signal:

    def __init__(self, sem, per):
        self.sem, self.per = sem, per

    def before(self, layer, g):
        return GROUPS * sum(self.per[:layer]) + g * self.per[layer]

    def at(self, layer, g, k=None):
        return self.before(layer, g) + (self.per[layer] if k is None else k)


class Count:

    def __init__(self, sig, layer, g, start=0):
        self.sem, self.first, self.n = sig.sem, sig.before(layer, g), start
        self.all = sig.per[layer]

    def one(self):
        self.n += 1
        return 1

    def value(self):
        return self.first + self.n

    def full(self):
        assert self.n == self.all, (self.n, self.all)


def due(value):
    return not isinstance(value, int) or value > 0


def span(start, size):
    return slice(start, start + size) if isinstance(start, int) else bass.ds(start, size)


COLS = [("l0_b1", 16), ("l0_b2", 8), ("l0_a", 2), ("l1_rb1", 1), ("l1_b1", 6), ("l1_b2", 6),
        ("l1_b3", 6), ("l2_bq", 1), ("l2_bk", 1), ("l2_mb1", 4), ("l2_b1", 32), ("l2_b2", 8),
        ("l2_lng", 8), ("l2_lnb", 8), ("l3_a", 2), ("l3_b1", 32), ("l3_b2", 8)]
ROWS = [("l0_bg", 8), ("l1_bg", 6), ("l2_bg", 8), ("l3_bg", 8), ("l1_bias", P), ("l2_bv", P),
        ("l2_bo", P), ("l2_g1", P), ("l2_c1", P), ("l2_mb2", P), ("l2_g2", P), ("l2_c2", P)]
MATS = [("l0_wT", P), ("l0_w", P), ("l0_wg", 8), ("l1_w", RELATIONS * P), ("l1_rw1", 64),
        ("l1_rw2", 6), ("l2_wq", P), ("l2_wk", P), ("l2_wv", P), ("l2_wo", P), ("l2_w1", 4 * P),
        ("l2_w2", 4 * P), ("l2_wg", 8), ("l3_w", P), ("l3_wT", P), ("l3_wg", 8)]


def places(table):
    at, out = 0, {}
    for name, n in table:
        out[name] = (at, n)
        at += n
    return out, at


COL_AT, N_COLS = places(COLS)
ROW_AT, N_ROWS = places(ROWS)
MAT_AT, N_MATS = places(MATS)

PREP_STEPS = {
    0: [(0, "p_norm"), (0, "p_apply"), (2, "p_turn"), (3, "p_split"), (3, "p_logits"), (4, "p_route"),
        (4, "p_weigh"), (6, "p_gates")],
    1: [(0, "p_norm"), (0, "p_apply"), (2, "p_turn"), (2, "p_split"), (2, "p_router"), (3, "p_logits"),
        (3, "p_route"), (4, "p_weigh"), (5, "p_gates")],
    2: [(0, "p_norm"), (0, "p_apply"), (1, "p_turn"), (1, "p_norm2"), (1, "p_apply2"), (2, "p_logits"),
        (2, "p_route"), (4, "p_weigh"), (4, "p_turn2"), (5, "p_split"), (6, "p_gates")],
    3: [(0, "p_norm"), (0, "p_apply"), (1, "p_turn"), (2, "p_split"), (2, "p_logits"), (3, "p_route"),
        (4, "p_weigh"), (6, "p_gates")],
}
GNN_STEPS = {
    0: [(1, "g_norm"), (1, "g_apply"), (3, "g_turn"), (4, "g_scores"), (5, "g_center"), (5, "g_exp"),
        (6, "g_turn_p"), (7, "g_mix"), (7, "g_add")],
    1: [(1, "g_norm"), (1, "g_apply"), (3, "g_rel0"), (4, "g_rel1"), (5, "g_mix"), (5, "g_add")],
    3: [(1, "g_norm"), (1, "g_apply"), (2, "g_turn"), (3, "g_scores"), (4, "g_center"), (5, "g_exp"),
        (6, "g_turn_p"), (7, "g_mix"), (7, "g_add")],
}


TRANSFORMER = [
    ("t_mix", -1, 3), ("t_mlp1", -2, 0), ("t_norm", 1, 0), ("t_pow", 1, 0), ("t_apply", 1, 0),
    ("t_turn_p", 0, 0), ("t_keys", 0, 2), ("t_turn_c", -1, 0), ("t_scores", 0, 1), ("t_mix", 0, 0),
    ("t_mlp1", -2, 1), ("t_out", -1, 0), ("t_turn", 1, 0), ("t_turn_p", 0, 1), ("t_pow", -1, 1),
    ("t_keys", 0, 3), ("t_scores", 0, 2), ("t_mix", 0, 1), ("t_project", 1, 0), ("t_norm1", -1, 0),
    ("t_turn_p", 0, 2), ("t_keys", 1, 0), ("t_scores", 0, 3), ("t_pow", -2, 2), ("t_mlp2", -2, 0),
    ("t_mix", 0, 2), ("t_mask", 1, 0), ("t_queries", 1, 0), ("t_turn_n", -1, 0), ("t_norm2", -2, 0),
    ("t_keys", 1, 1), ("t_turn_p", 0, 3), ("t_scores", 1, 0),
]


ROUTE_FIRST = {
    (GROUPS, "t_mix", -1, 3): ["p_norm", "p_apply"],
    (GROUPS, "t_mlp1", -2, 0): ["p_turn", "p_norm2", "p_apply2"],
    (GROUPS, "t_mlp1", -2, 1): ["p_logits"],
    (GROUPS, "t_norm1", -1, 0): ["p_route"],
    (GROUPS, "t_turn_n", -1, 0): ["p_weigh", "p_turn2"],
    (GROUPS, "t_norm2", -2, 0): ["p_split"],
    (GROUPS + 1, "t_mlp1", -2, 1): ["p_gates"],
}


def steps_at(table, slot):
    return [name for at, name in table if at == slot]


def side_order(layer, g, slot):
    last = isinstance(g, int) and g >= GROUPS - 2
    out = []
    nxt = (layer, g + 1) if not (isinstance(g, int) and g == GROUPS - 1) else (layer + 1, 0)
    if nxt[0] < LAYERS and nxt[0] != 2 or nxt[0] == layer:
        out += [(name, *nxt) for name in steps_at(PREP_STEPS[nxt[0]], slot)]
    target = (layer, g + 2) if not last else (layer + 1, g - (GROUPS - 2))
    if target[0] in GNN_STEPS:
        out += [(name, *target) for name in steps_at(GNN_STEPS[target[0]], slot)]
    if layer == 1 and isinstance(g, int) and g == GROUPS - 1:
        out += [("w2_bias", 2, 0)] * (slot == 2) + [("w2_split", 2, slot - 3)] * (slot >= 3)
    if layer == 2 and isinstance(g, int) and g == GROUPS - 1:
        out += [("w3_split", 3, slot - 2)] * (slot >= 2)
    if layer == 3 and isinstance(g, int) and g == 0:
        out += [("w3_split", 3, slot + 6)] * (slot < 2)
    out.sort(key=lambda step: "apply" in step[0])
    return out


def build(nc, x, adj, adjT, mats, cols, rows, l0_w1, l0_w2, l1_w1, l1_w2, l1_w3,
          l2_w1, l2_w2, l3_w1, l3_w2, out):
    with ExitStack() as ctx:
        def sb(name, shape, dt=F32):
            return ctx.enter_context(nc.sbuf_tensor(name, shape, dt))

        def ps(name, banks=1):
            return ctx.enter_context(nc.psum_tensor(name, [P, banks * TOK], F32))

        def signal(name, *per):
            return Signal(ctx.enter_context(nc.semaphore(name)), list(per))

        def sem(name):
            return ctx.enter_context(nc.semaphore(name))

        X = sb("X", [P, GRAPHS * P])
        ADJ = sb("ADJ", [P, 2 * TOK], I32)
        MATW = sb("MATW", [P, N_MATS])
        COLW = sb("COLW", [P, N_COLS])
        ROWW = sb("ROWW", [P, N_ROWS])
        W = sb("W", [P, 16384], F32R)
        RINGS = sb("RINGS", [P, 4096])
        HH = sb("HH", [P, HB * TOK], F32R)
        HL = sb("HL", [P, HB * TOK], F32R)
        V = sb("V", [P, 4 * P])
        IDF = sb("IDF", [P, P])
        IDB = sb("IDB", [P, P], BF16)
        SEL = sb("SEL", [24, 8 * P], BF16)
        IOTA = sb("IOTA", [P, 8])
        POW = sb("POW", [P, 4])
        HM = sb("HM", [P, HEADS])
        LNB1 = sb("LNB1", [P, 32])
        H = sb("H", [P, HB * TOK])
        XH = sb("XH", [P, 2 * TOK], F32R)
        XL = sb("XL", [P, 2 * TOK], F32R)
        GT = sb("GT", [24, 2 * TOK], BF16)
        WORK = sb("WORK", [P, 8 * TOK])
        GS = WORK[:, 0:2 * TOK]
        T = WORK[:, 2 * TOK:4 * TOK]
        ACC = WORK[:, 4 * TOK:5 * TOK]
        PT = WORK[:, 5 * TOK:6 * TOK]
        PX = WORK[:, 6 * TOK:7 * TOK]
        PX2 = WORK[:, 7 * TOK:8 * TOK]
        ST = sb("ST", [P, 4 * 6])
        MV = sb("MV", [P, 4 * 2])
        RS = sb("RS", [P, 4])
        GST = sb("GST", [P, 4 * 6])
        GMV = sb("GMV", [P, 4 * 2])
        GRS = sb("GRS", [P, 4])
        RT = sb("RT", [P, 12 * 32])
        RV = sb("RV", [P, 12 * 4])
        GB3 = sb("GB3", [P, 4 * 24], BF16)
        PEN = sb("PEN", [P, TOK], BF16)
        NEB = sb("NEB", [P, P], BF16)
        BQ4 = sb("BQ4", [P, 1])
        SCR = sb("SCR", [P, 4608])

        def col(name, i=0):
            return COLW[:, COL_AT[name][0] + i:COL_AT[name][0] + i + 1]

        def row(name):
            return ROWW[:, ROW_AT[name][0]:ROW_AT[name][0] + ROW_AT[name][1]]

        def mat(name, i=0, n=None):
            at, width = MAT_AT[name]
            return MATW[:, at + i:at + i + (n or width)]

        def x_at(g):
            return X[:, span(g * TOK, TOK)]

        def half(t, g, rows_=P):
            return t[0:rows_, span((g % 2) * TOK, TOK)]

        def graphs(ap, n=P):
            return ap.rearrange("p (b n) -> p b n", n=n)

        W1 = {0: (0, 2048), 1: (8192, 768), 2: (0, 4096), 3: (0, 4096)}
        W2_HI, W2_LO = 8192, 12288
        W2_L0, W2_L1, W3_L1 = (RINGS[:, at:at + n] for at, n in ((0, 2048), (2048, 768), (2816, 768)))
        W3_STAGE = [RINGS[:, 2048:3072], RINGS[:, 3072:4096]]

        ZZ, YY, QQ = ps("ZZ", 2), ps("YY", 2), ps("QQ", 2)
        Z = [ZZ[:, 0:TOK], ZZ[:, TOK:2 * TOK]]
        Y = [YY[:, 0:TOK], YY[:, TOK:2 * TOK]]
        GB, PA = QQ[:, 0:TOK], QQ[:, TOK:2 * TOK]
        PB, PC = ps("PB"), ps("PC")

        x_first, x_rest = sem("x_first"), sem("x_rest")
        small_in = sem("small_in")
        w1_in, w2_in = sem("w1_in"), sem("w2_in")
        l2_in = sem("l2_in")
        l3_split = sem("l3_split")
        l3_in = [sem("l3_in_even"), sem("l3_in_odd")]
        consts = sem("consts")
        w_split = sem("w_split")
        v_mm, v_done = sem("v_mm"), sem("v_done")
        stored = sem("stored")
        adj_in = signal("adj_in", 16, 16, 32, 16)
        z_full = signal("z_full", *JOBS)
        h_done = signal("h_done", *JOBS)
        h_hi = signal("h_hi", 0, 0, 32, 32)
        h_lo_first = signal("h_lo_first", 0, 0, 8, 8)
        h_lo_rest = signal("h_lo_rest", 0, 0, 24, 24)
        y_full = signal("y_full", *EXPERTS)
        g_full = signal("g_full", *EXPERTS)
        gs_done = signal("gs_done", *EXPERTS)
        comb = signal("comb", *EXPERTS)
        acc_done = signal("acc_done", *[e - 1 for e in EXPERTS])
        tail_tr = signal("tail_tr", 1, 1, 1, 1)
        tail_x = signal("tail_x", 1, 1, 1, 1)
        p_ln = signal("p_ln", 13, 13, 26, 13)
        p_rs = signal("p_rs", 1, 1, 2, 1)
        g_rs = signal("g_rs", 1, 1, 0, 1)
        p_tr = signal("p_tr", 1, 1, 2, 1)
        p_ev = signal("p_ev", 1, 1, 2, 1)
        p_sp = signal("p_sp", 2, 2, 2, 2)
        p_r1 = signal("p_r1", 0, 1, 0, 0)
        p_rh = signal("p_rh", 0, 1, 0, 0)
        p_lg = signal("p_lg", 1, 1, 1, 1)
        p_dv = signal("p_dv", 17, 28, 23, 23)
        p_ex = signal("p_ex", 0, 2, 1, 1)
        p_gt = signal("p_gt", 1, 1, 1, 1)
        p_ge = signal("p_ge", 1, 1, 1, 1)
        g_ln = signal("g_ln", 13, 13, 0, 13)
        g_pen = signal("g_pen", 1, 4, 0, 1)
        g_tr = signal("g_tr", 1, 2, 0, 1)
        g_ev = signal("g_ev", 1, 4, 0, 1)
        g_sc = signal("g_sc", 1, 0, 0, 1)
        g_se = signal("g_se", 2, 0, 0, 1)
        g_ce = signal("g_ce", 3, 0, 0, 2)
        g_ex = signal("g_ex", 1, 0, 0, 1)
        g_pt = signal("g_pt", 1, 0, 0, 1)
        g_su = signal("g_su", 2, 0, 0, 2)
        g_pe = signal("g_pe", 1, 0, 0, 1)
        g_mx = signal("g_mx", 1, 1, 0, 1)
        g_ad = signal("g_ad", 2, 2, 0, 4)
        g_el = signal("g_el", 0, 0, 0, 1)

        t_ln = signal("t_ln", 0, 0, 14, 0)
        t_rw = [signal("t_rw0", 0, 0, 1, 0), signal("t_rw1", 0, 0, 1, 0), signal("t_rw2", 0, 0, 1, 0)]
        t_tr = signal("t_tr", 0, 0, 1, 0)
        t_ut = signal("t_ut", 0, 0, 1, 0)
        t_qkv = signal("t_qkv", 0, 0, 3, 0)
        t_kt = signal("t_kt", 0, 0, 1, 0)
        t_qt = signal("t_qt", 0, 0, 1, 0)
        t_ve = signal("t_ve", 0, 0, 1, 0)
        t_pen = signal("t_pen", 0, 0, 2, 0)
        t_km = signal("t_km", 0, 0, 4, 0)
        t_sc = signal("t_sc", 0, 0, 4, 0)
        t_ce = signal("t_ce", 0, 0, 8, 0)
        t_ex = signal("t_ex", 0, 0, 4, 0)
        t_tp = signal("t_tp", 0, 0, 4, 0)
        t_pe = signal("t_pe", 0, 0, 4, 0)
        t_pv = signal("t_pv", 0, 0, 4, 0)
        t_cx = signal("t_cx", 0, 0, 8, 0)
        t_ct = signal("t_ct", 0, 0, 1, 0)
        t_cv = signal("t_cv", 0, 0, 1, 0)
        t_wo = signal("t_wo", 0, 0, 1, 0)
        t_n1 = signal("t_n1", 0, 0, 18, 0)
        t_t1 = signal("t_t1", 0, 0, 1, 0)
        t_nt = signal("t_nt", 0, 0, 1, 0)
        t_m1 = signal("t_m1", 0, 0, 4, 0)
        t_mh = signal("t_mh", 0, 0, 4, 0)
        t_m2 = signal("t_m2", 0, 0, 1, 0)
        t_x = signal("t_x", 0, 0, 17, 0)
        w_bias = sem("w_bias")
        l2_consts = sem("l2_consts")

        TE = SCR[:, 0:1024]
        TPT = SCR[:, 1024:2048]
        TKM = [SCR[:, 2048:3072], SCR[:, 3072:4096]]
        TQT = SCR[:, 4096:4608]
        TU_RING, TKT_RING, TNB_RING = RINGS[:, 0:2048], RINGS[:, 2048:3072], RINGS[:, 3072:4096]
        TVE = WORK[:, 0:1088]
        TC = WORK[:, 1088:1600]
        TT = WORK[:, 1600:2112]
        TNT = WORK[:, 2112:2624]
        TU = WORK[:, 2624:3136]
        TN1 = WORK[:, 3136:3648]
        TM = WORK[:, 3648:3904].bitcast(BF16)
        TR2 = TU
        ST2, MV2 = RT[:, 0:24], RT[:, 24:32]
        TRC = RV[:, 0:8]
        VE_ROW = HEADS * (HD + 1)

        GXN = SCR[:, 0:512]
        GXT = SCR[:, 512:1024]
        GH = SCR[:, 1024:1536]
        GZ = SCR[:, 1536:2048]
        GE = SCR[:, 2048:2560]
        GP = SCR[:, 2560:3072]
        GPT = SCR[:, 3072:3584]
        GR = SCR[:, 3584:3600]
        GM = SCR[:, 512:2560]
        GHT = SCR[:, 2560:4608]

        def early(layer, g):
            return layer == 2 and isinstance(g, int) and g == 0

        def px(layer, g):
            return RINGS[:, 2048:2560] if early(layer, g) else PX

        def px2(layer, g):
            return RINGS[:, 2560:3072] if early(layer, g) else PX2

        def pt(layer, g):
            return RINGS[:, 1024:1536] if early(layer, g) else PT

        block = ctx.enter_context(nc.Block())

        class Walk:

            def __init__(self, eng, slot, tail, steps, begin, ahead):
                self.eng, self.slot, self.tail, self.steps = eng, slot, tail, steps
                self.begin, self.ahead = begin, ahead

            def group(self, layer, g):
                if layer == 1 and isinstance(g, int) and g == 0:
                    self.slot(layer, g, -1)
                for s in range(SLOTS[layer]):
                    self.slot(layer, g, s)
                    if s == 0 and not (layer == 0 and isinstance(g, int) and g == 0) \
                            and not (layer == 2 and isinstance(g, int) and g == 0):
                        self.tail(*((layer, g - 1) if not (isinstance(g, int) and g == 0)
                                    else (layer - 1, GROUPS - 1)))
                    for name, la, gr in side_order(layer, g, s):
                        if name in self.steps:
                            self.steps[name](la, gr)

            def alone(self, table, layer, g):
                for _, name in table[layer]:
                    if name in self.steps:
                        self.steps[name](layer, g)

            def transformer(self, g):
                for name, ahead, b in TRANSFORMER:
                    if not isinstance(g, int) or 0 <= g + ahead < GROUPS:
                        if name in self.steps:
                            self.steps[name](g + ahead, b)
                        if not isinstance(g, int):
                            continue
                        if g == -1 and name == "t_apply":
                            self.tail(1, GROUPS - 1)
                        for first in ROUTE_FIRST.get((g, name, ahead, b), ()):
                            if first in self.steps:
                                self.steps[first](2, 0)

            def run(self):
                self.begin()
                self.alone(GNN_STEPS, 0, 0)
                for s in range(SLOTS[0]):
                    for name, la, gr in side_order(0, -1, s):
                        if name in self.steps:
                            self.steps[name](la, gr)
                self.ahead(0)
                for layer in range(LAYERS):
                    if layer == 2:
                        for g in (-1, 0, 1, 2):
                            self.transformer(g)
                        with self.eng.Fori(3, GROUPS - 1) as g:
                            self.transformer(g)
                        for g in (GROUPS - 1, GROUPS, GROUPS + 1):
                            self.transformer(g)
                        self.ahead(2)
                    self.group(layer, 0)
                    with self.eng.Fori(1, GROUPS - 2) as g:
                        self.group(layer, g)
                    self.group(layer, GROUPS - 2)
                    self.group(layer, GROUPS - 1)
                self.tail(LAYERS - 1, GROUPS - 1)

        def follows(layer, g):
            return not (isinstance(g, int) and g == GROUPS - 1 and layer in (1, 3))

        def job_at(layer, g, job):
            if job < JOBS[layer]:
                return layer, g, job
            if isinstance(g, int) and g == GROUPS - 1:
                return layer + 1, 0, job - JOBS[layer]
            return layer, g + 1, job - JOBS[layer]

        @block.sync
        def _(sp):
            x_in = x.rearrange("b n d -> n b d")
            x_out = out.rearrange("b n d -> n b d")
            XV = X[:, :].rearrange("p (b d) -> p b d", d=P)
            adj_v = adj.rearrange("b i j -> i b j")
            adjT_v = adjT.rearrange("b i j -> i b j")

            def load_adj(layer, g):
                if layer == 3 and isinstance(g, int) and g < 2:
                    sp.wait_ge(t_pen.sem, t_pen.at(2, GROUPS - 1))
                elif layer or not isinstance(g, int) or g >= 2:
                    la, gr = (layer, g - 2) if not (isinstance(g, int) and g < 2) else (layer - 1, GROUPS - 2 + g)
                    sp.wait_ge(g_pen.sem, g_pen.at(la, gr))
                if due(adj_in.before(layer, g)):
                    sp.wait_ge(adj_in.sem, adj_in.before(layer, g))
                if layer == 2:
                    return
                src = adjT_v if layer == 1 else adj_v
                sp.dma_start(graphs(half(ADJ, g)), src[:, span(g * PER_GROUP, PER_GROUP), :])\
                    .then_inc(adj_in.sem, 16)

            sp.dma_start(XV[:, 0:8, :], x_in[:, 0:8, :]).then_inc(x_first, 16)
            load_adj(0, 0)
            load_adj(0, 1)
            sp.dma_start(H[:, :], l0_w1).then_inc(w1_in, 16)
            sp.dma_start(T[:, 0:768], l1_w1).then_inc(w1_in, 16)
            sp.dma_start(W2_L0, l0_w2).then_inc(w2_in, 16)
            sp.dma_start(W2_L1, l1_w2).then_inc(w2_in, 16)
            sp.dma_start(W3_L1, l1_w3).then_inc(w2_in, 16)
            sp.dma_start(XV[:, 8:GRAPHS, :], x_in[:, 8:GRAPHS, :]).then_inc(x_rest, 16)

            def load_both(g):
                if due(t_pen.before(2, g)):
                    sp.wait_ge(t_pen.sem, t_pen.before(2, g))
                for n, src in enumerate((adj_v, adjT_v)):
                    sp.dma_start(graphs(ADJ[:, n * TOK:(n + 1) * TOK]),
                                 src[:, span(g * PER_GROUP, PER_GROUP), :]).then_inc(adj_in.sem, 16)

            for layer in range(LAYERS):
                if layer == 2:
                    sp.wait_ge(g_ad.sem, g_ad.at(1, GROUPS - 1))
                    sp.dma_start(SCR[:, 0:4096], l2_w1).then_inc(l2_in, 16)
                    sp.wait_ge(g_pen.sem, g_pen.at(1, GROUPS - 1))
                    if due(adj_in.before(2, 0)):
                        sp.wait_ge(adj_in.sem, adj_in.before(2, 0))
                    load_both(0)
                    with sp.Fori(1, GROUPS) as g:
                        load_both(g)
                    sp.wait_ge(t_pv.sem, t_pv.at(2, GROUPS - 1))
                    sp.dma_start(SCR[:, 0:4096], l2_w2).then_inc(l2_in, 16)
                    sp.wait_ge(t_x.sem, t_x.at(2, GROUPS - 1))
                    continue
                if layer:
                    for g in (0, 1):
                        load_adj(layer, g)
                if layer == 3:
                    sp.wait_ge(p_tr.sem, p_tr.at(2, 0))
                    sp.wait_ge(p_sp.sem, p_sp.at(2, 0))
                    for e in range(EXPERTS[3]):
                        if e > 1:
                            sp.wait_ge(l3_split, 4 * (e - 1))
                        stage, at = W3_STAGE[e % 2], e * 4 * P
                        sp.dma_start(stage[:, 0:4 * P], l3_w1[:, at:at + 4 * P]).then_inc(l3_in[e % 2], 16)
                        sp.dma_start(stage[:, 4 * P:8 * P], l3_w2[:, at:at + 4 * P]).then_inc(l3_in[e % 2], 16)
                with sp.Fori(1, GROUPS - 1) as g:
                    load_adj(layer, g + 1)
            with sp.Fori(0, GROUPS) as g:
                sp.wait_ge(tail_x.sem, tail_x.at(LAYERS - 1, g))
                sp.dma_start(x_out[:, span(g * PER_GROUP, PER_GROUP), :],
                             XV[:, span(g * PER_GROUP, PER_GROUP), :]).then_inc(stored, 16)
            sp.wait_ge(stored, 16 * GROUPS)

        @block.gpsimd
        def _(pool):
            def link(ins, sem_, count=[0]):
                count[0] += 1
                ins.then_inc(sem_, 1)
                pool.wait_ge(sem_, count[0])

            link(pool.memset(IDF[:, :], 0.0), consts)
            link(pool.affine_select(out=IDF[:, :], in_=IDF[:, :], compare_op=ALU.not_equal, fill=1.0,
                                    base=0, pattern=[[-1, P]], channel_multiplier=1), consts)
            link(pool.memset(IDB[:, :], 0.0), consts)
            link(pool.affine_select(out=IDB[:, :], in_=IDB[:, :], compare_op=ALU.not_equal, fill=1.0,
                                    base=0, pattern=[[-1, P]], channel_multiplier=1), consts)
            link(pool.memset(SEL[:, :], 0.0), consts)
            sel = SEL[:, :].rearrange("p (e n) -> p e n", n=P)
            for part in range(3):
                link(pool.affine_select(out=sel, in_=sel, compare_op=ALU.not_equal, fill=1.0,
                                        base=-8 * part, pattern=[[-1, 8], [0, P]], channel_multiplier=1), consts)
            for e in range(8):
                link(pool.memset(IOTA[:, e:e + 1], 64.0 + e), consts)
            link(pool.memset(POW[:, :], -0.5), consts)
            link(pool.memset(NEB[:, :], BARRED), consts)
            link(pool.affine_select(out=NEB[:, :], in_=NEB[:, :], compare_op=ALU.not_equal, fill=0.0,
                                    base=0, pattern=[[-1, P]], channel_multiplier=1), consts)
            link(pool.memset(HM[:, :], 1.0), consts)
            link(pool.affine_select(out=HM[:, :], in_=HM[:, :], compare_op=ALU.is_ge, fill=0.0,
                                    base=0, pattern=[[-HD, HEADS]], channel_multiplier=1), consts)
            link(pool.affine_select(out=HM[:, :], in_=HM[:, :], compare_op=ALU.is_ge, fill=0.0,
                                    base=HD - 1, pattern=[[HD, HEADS]], channel_multiplier=-1), consts)

            def hidden_lo(layer, g, job):
                if layer < 2 or not follows(layer, g) and job >= JOBS[layer]:
                    return
                layer, g, job = job_at(layer, g, job)
                if job % 4 == 0:
                    return
                pool.wait_ge(h_hi.sem, h_hi.at(layer, g, job + 1))
                at = (job % HB) * TOK
                pool.tensor_tensor(HL[:, at:at + TOK], H[:, at:at + TOK], HH[:, at:at + TOK].bitcast(F32),
                                   ALU.subtract).then_inc(h_lo_rest.sem, 1)

            def slot(layer, g, e):
                if e < 0:
                    return
                for k in range(BLOCKS[layer]):
                    hidden_lo(layer, g, e * BLOCKS[layer] + k + AHEAD[layer])
                    if k == 0:
                        if e > 1:
                            add(layer, g, e - 1)
                        elif e == 0 and layer in (1, 3) and isinstance(g, int) and g == 0:
                            add(layer - 1, GROUPS - 1, EXPERTS[layer - 1] - 1)
                        elif e == 0 and not (isinstance(g, int) and g == 0):
                            add(layer, g - 1, EXPERTS[layer] - 1)

            def add(layer, g, e):
                pool.wait_ge(comb.sem, comb.at(layer, g, e + 1))
                if e > 1:
                    pool.wait_ge(acc_done.sem, acc_done.at(layer, g, e - 1))
                pool.tensor_tensor(ACC[:, :], ACC[:, :], T[:, (e % 2) * TOK:(e % 2 + 1) * TOK],
                                   ALU.add).then_inc(acc_done.sem, 1)

            def tail(layer, g):
                if isinstance(g, int) and g == GROUPS - 1 and layer in (1, 3):
                    add(layer, g, EXPERTS[layer] - 1)

            def p_apply(layer, g):
                pool.wait_ge(p_ln.sem, p_ln.at(layer, g, 9))
                pool.tensor_tensor(RS[:, :], RS[:, :], POW[:, :], ALU.pow).then_inc(p_rs.sem, 1)

            def p_apply2(layer, g):
                pool.wait_ge(p_ln.sem, p_ln.at(layer, g, 22))
                pool.tensor_tensor(RS[:, :], RS[:, :], POW[:, :], ALU.pow).then_inc(p_rs.sem, 1)

            def g_apply(layer, g):
                pool.wait_ge(g_ln.sem, g_ln.at(layer, g, 9))
                pool.tensor_tensor(GRS[:, :], GRS[:, :], POW[:, :], ALU.pow).then_inc(g_rs.sem, 1)

            def t_pow(g, n):
                source = (t_ln, t_n1, t_x)[n]
                pool.wait_ge(source.sem, source.at(2, g, (9, 11, 10)[n]))
                r = (GRS, RS, RV[:, 12:16])[n]
                pool.tensor_tensor(r[:, 0:4], r[:, 0:4], POW[:, :], ALU.pow).then_inc(t_rw[n].sem, 1)

            def t_keys(g, b):
                pool.wait_ge(t_kt.sem, t_kt.at(2, g))
                if due(t_sc.before(2, g) + b - 1):
                    pool.wait_ge(t_sc.sem, t_sc.before(2, g) + b - 1)
                keys = TKT_RING[:, span((g % 2) * TOK + b * P, P)]
                pool.tensor_tensor(TKM[b % 2].rearrange("p (h n) -> p h n", n=P),
                                   keys.unsqueeze(1).to_broadcast([P, HEADS, P]),
                                   HM[:, :].unsqueeze(2).to_broadcast([P, HEADS, P]), ALU.mult)\
                    .then_inc(t_km.sem, 1)

            Walk(pool, slot, tail,
                 dict(t_pow=t_pow, t_keys=t_keys, p_apply=p_apply, p_apply2=p_apply2, g_apply=g_apply), lambda: None,
                 lambda layer: [hidden_lo(layer, 0, job) for job in range(AHEAD[layer])]).run()

        N_CONSTS = 22

        @block.tensor
        def _(pe):
            def turn(dst, src):
                for b in range(PER_GROUP):
                    last = pe.transpose(dst[:, b * P:(b + 1) * P], src[:, b * P:(b + 1) * P], IDF[:, :])
                return last

            def up(layer, g, job):
                if not follows(layer, g) and job >= JOBS[layer]:
                    return
                layer, g, job = job_at(layer, g, job)
                if layer == 3 and isinstance(g, int) and g == 0 and job % 4 == 0:
                    pe.wait_ge(l3_split, 4 * (job // 4 + 1))
                if job == 0:
                    pe.wait_ge(p_sp.sem, p_sp.at(layer, g))
                read = h_hi if layer > 1 else h_done
                if due(read.before(layer, g) + job - 1):
                    pe.wait_ge(read.sem, read.before(layer, g) + job - 1)
                z = Z[job % 2]
                at, n = W1[layer]
                if layer == 1 and job not in L1_FIRST:
                    e = L1_SECOND.index(job)
                    pe.wait_ge(h_done.sem, h_done.at(1, g, L1_FIRST[e] + 1))
                    last = pe.matmul(z[:, :], W2_L1[:, e * P:(e + 1) * P],
                                     hidden(L1_FIRST[e]), start=True, stop=True)
                else:
                    e = L1_FIRST.index(job) if layer == 1 else job
                    hi = W[:, at + e * P:at + (e + 1) * P]
                    lo = W[:, at + n + e * P:at + n + (e + 1) * P]
                    pe.matmul(z[:, :], lo, half(XH, g), start=True, stop=False)
                    pe.matmul(z[:, :], hi, half(XL, g), start=False, stop=False)
                    last = pe.matmul(z[:, :], hi, half(XH, g), start=False, stop=True)
                last.then_inc(z_full.sem, 1)

            def hidden(job):
                return H[:, (job % HB) * TOK:(job % HB + 1) * TOK]

            def gates_free(layer, g, e):
                if e == 0:
                    pe.wait_ge(p_ge.sem, p_ge.at(layer, g))
                if due(gs_done.before(layer, g) + e):
                    pe.wait_ge(gs_done.sem, gs_done.before(layer, g) + e)

            def gates(layer, g, e):
                pe.matmul(GB[:, :], SEL[:, e * P:(e + 1) * P], half(GT, g, 24), start=True, stop=True)\
                    .then_inc(g_full.sem, 1)

            def slot(layer, g, e):
                if e < 0:
                    up(layer, g, 2)
                    return
                nb = BLOCKS[layer]
                y = Y[e % 2]
                if due(comb.before(layer, g) + e - 1):
                    pe.wait_ge(comb.sem, comb.before(layer, g) + e - 1)
                if layer == 1:
                    gates_free(layer, g, e)
                    pe.wait_ge(h_done.sem, h_done.at(1, g, L1_SECOND[e] + 1))
                    pe.matmul(y[:, :], W3_L1[:, e * P:(e + 1) * P], hidden(L1_SECOND[e]),
                              start=True, stop=True).then_inc(y_full.sem, 1)
                    gates(layer, g, e)
                    up(layer, g, 2 * e + 3)
                    up(layer, g, 2 * e + 4)
                    return
                for k in range(nb):
                    job = e * nb + k
                    if layer == 2 and isinstance(g, int) and g == 0 and job == 0:
                        pe.wait_ge(w_split, 8)
                    if k == 0:
                        gates_free(layer, g, e)
                    if layer > 1:
                        hh, hl = (t[:, (job % HB) * TOK:(job % HB + 1) * TOK] for t in (HH, HL))
                        hi = W[:, W2_HI + job * P:W2_HI + (job + 1) * P]
                        pe.wait_ge(h_hi.sem, h_hi.at(layer, g, job + 1))
                        pe.matmul(y[:, :], W[:, W2_LO + job * P:W2_LO + (job + 1) * P], hh, start=(k == 0), stop=False)
                        pe.matmul(y[:, :], hi, hh, start=False, stop=False)
                        if k == 0:
                            pe.wait_ge(h_lo_first.sem, h_lo_first.at(layer, g, e + 1))
                        else:
                            pe.wait_ge(h_lo_rest.sem, h_lo_rest.at(layer, g, 3 * e + k))
                        last = pe.matmul(y[:, :], hi, hl, start=False, stop=(k == nb - 1))
                    else:
                        pe.wait_ge(h_done.sem, h_done.at(layer, g, job + 1))
                        last = pe.matmul(y[:, :], W2_L0[:, job * P:(job + 1) * P], hidden(job),
                                         start=(k == 0), stop=(k == nb - 1))
                    if k == nb - 1:
                        last.then_inc(y_full.sem, 1)
                    if k == 0:
                        gates(layer, g, e)
                    up(layer, g, job + AHEAD[layer])

            def tail(layer, g):
                pe.wait_ge(acc_done.sem, acc_done.at(layer, g))
                turn(PC, ACC).then_inc(tail_tr.sem, 1)

            def p_turn(layer, g):
                pe.wait_ge(p_ln.sem, p_ln.at(layer, g, 13))
                if early(layer, g):
                    pe.wait_ge(t_cx.sem, t_cx.at(2, GROUPS - 1))
                if layer != 0 or not (isinstance(g, int) and g == 0):
                    if due(tail_x.before(layer, g) - 1):
                        pe.wait_ge(tail_x.sem, tail_x.before(layer, g) - 1)
                    if due(p_ge.before(layer, g)):
                        pe.wait_ge(p_ge.sem, p_ge.before(layer, g))
                turn(PC, px(layer, g)).then_inc(p_tr.sem, 1)

            def p_router(layer, g):
                pe.wait_ge(p_ev.sem, p_ev.at(layer, g))
                pe.matmul(PC[0:64, :], mat("l1_rw1"), pt(layer, g)[:, :], start=True, stop=True).then_inc(p_r1.sem, 1)

            def p_logits(layer, g):
                if layer == 1:
                    pe.wait_ge(p_rh.sem, p_rh.at(layer, g))
                    for b in range(PER_GROUP):
                        last = pe.matmul(PC[:, b * 8:b * 8 + 6], PX[0:64, b * P:(b + 1) * P],
                                         mat("l1_rw2")[0:64, :], start=True, stop=True)
                else:
                    pe.wait_ge(p_ev.sem, p_ev.at(layer, g, 1))
                    for b in range(PER_GROUP):
                        last = pe.matmul(PC[:, b * 8:b * 8 + 8], pt(layer, g)[:, b * P:(b + 1) * P],
                                         mat(f"l{layer}_wg"), start=True, stop=True)
                last.then_inc(p_lg.sem, 1)

            def p_gates(layer, g):
                pe.wait_ge(p_dv.sem, p_dv.at(layer, g))
                pe.wait_ge(p_ev.sem, p_ev.at(layer, g))
                gt = PC[:, 0:TOK // 2].bitcast(BF16)
                for b in range(PER_GROUP):
                    last = pe.transpose(gt[0:24, b * P:(b + 1) * P], GB3[:, b * 24:(b + 1) * 24], IDB[:, :])
                last.then_inc(p_gt.sem, 1)

            def g_turn(layer, g):
                pe.wait_ge(g_ln.sem, g_ln.at(layer, g))
                turn(PA, GXN).then_inc(g_tr.sem, 1)

            def g_scores(layer, g):
                pe.wait_ge(g_ev.sem, g_ev.at(layer, g))
                pe.wait_ge(g_pen.sem, g_pen.at(layer, g))
                w = mat("l0_wT") if layer == 0 else mat("l3_w")
                v = 0 if layer == 0 else 2 * P
                for b in range(PER_GROUP):
                    pe.matmul(PB[:, b * P:(b + 1) * P], GXT[:, b * P:(b + 1) * P], w, start=True, stop=True)
                pe.matmul(PA[:, :], V[:, v + P:v + 2 * P], GXT, start=True, stop=False, skip_group_check=True)
                for b in range(PER_GROUP):
                    pe.matmul(PA[:, b * P:(b + 1) * P], GXT[:, b * P:(b + 1) * P], V[:, v:v + P],
                              start=False, stop=False, skip_group_check=True)
                pe.matmul(PA[:, :], IDB[:, :], PEN[:, :], start=False, stop=True, skip_group_check=True)\
                    .then_inc(g_sc.sem, 1)

            def g_turn_p(layer, g):
                pe.wait_ge(g_ex.sem, g_ex.at(layer, g))
                turn(PA, GP).then_inc(g_pt.sem, 1)

            def g_mix(layer, g):
                if layer == 1:
                    pe.wait_ge(g_ev.sem, g_ev.at(layer, g))
                    for b in range(PER_GROUP):
                        for r in range(RELATIONS):
                            at = (b * RELATIONS + r) * P
                            last = pe.matmul(PA[:, b * P:(b + 1) * P], GHT[:, at:at + P],
                                             mat("l1_w", r * P, P), start=(r == 0), stop=(r == RELATIONS - 1))
                else:
                    pe.wait_ge(g_pe.sem, g_pe.at(layer, g))
                    for b in range(PER_GROUP):
                        last = pe.matmul(PB[:, b * P:(b + 1) * P], GPT[:, b * P:(b + 1) * P],
                                         GH[:, b * P:(b + 1) * P], start=True, stop=True)
                last.then_inc(g_mx.sem, 1)

            def relations(layer, g, pair):
                pe.wait_ge(g_ln.sem, g_ln.at(layer, g))
                pe.wait_ge(g_pen.sem, g_pen.at(layer, g))
                if pair:
                    pe.wait_ge(g_ev.sem, g_ev.at(layer, g, 2))
                for b, bank in ((2 * pair, PA), (2 * pair + 1, PB)):
                    last = pe.matmul(bank[:, :], GXN[:, b * P:(b + 1) * P],
                                     GM[:, b * RELATIONS * P:(b + 1) * RELATIONS * P], start=True, stop=True)
                last.then_inc(g_tr.sem, 1)

            def p_turn2(layer, g):
                pe.wait_ge(p_ln.sem, p_ln.at(layer, g))
                pe.wait_ge(p_dv.sem, p_dv.at(layer, g, 1))
                turn(PC, px2(layer, g)).then_inc(p_tr.sem, 1)

            def w2_bias(layer, g):
                pe.wait_ge(l2_in, 16)
                for e in range(8):
                    for k in range(4):
                        at = (e * 4 + k) * P
                        last = pe.matmul(PA[:, e * 4 + k:e * 4 + k + 1], SCR[:, at:at + P],
                                         col("l2_lnb", e), start=True, stop=True)
                last.then_inc(w_bias, 1)

            def t_turn(g, b):
                pe.wait_ge(t_ln.sem, t_ln.at(2, g))
                if due(t_mh.before(2, g) - 8):
                    pe.wait_ge(t_mh.sem, t_mh.before(2, g) - 8)
                turn(Y[0], TU).then_inc(t_tr.sem, 1)

            def t_project(g, b):
                pe.wait_ge(t_ut.sem, t_ut.at(2, g))
                pe.matmul(Y[0], mat("l2_wk"), TT, start=True, stop=True).then_inc(t_qkv.sem, 1)
                if due(t_mh.before(2, g) - 8):
                    pe.wait_ge(t_mh.sem, t_mh.before(2, g) - 8)
                pe.matmul(Y[1], mat("l2_wq"), TT, start=True, stop=True).then_inc(t_qkv.sem, 1)
                if due(t_n1.before(2, g) - 36 + 1 if not isinstance(g, int) or g >= 2 else 0):
                    pe.wait_ge(t_n1.sem, t_n1.before(2, g) - 36 + 1 if not isinstance(g, int) or g >= 2 else 0)
                for n in range(PER_GROUP):
                    last = pe.matmul(PB[:, n * P:(n + 1) * P], TT[:, n * P:(n + 1) * P], mat("l2_wv"),
                                     start=True, stop=True)
                last.then_inc(t_qkv.sem, 1)

            def t_scores(g, b):
                if b == 0:
                    pe.wait_ge(t_qt.sem, t_qt.at(2, g))
                    pe.wait_ge(t_pen.sem, t_pen.at(2, g))
                pe.wait_ge(t_km.sem, t_km.at(2, g, b + 1))
                if due(t_ce.before(2, g) + 2 * b):
                    pe.wait_ge(t_ce.sem, t_ce.before(2, g) + 2 * b)
                mask = PEN[:, b * P:(b + 1) * P].unsqueeze(1).to_broadcast([P, 4, P])
                for n in range(2):
                    pe.matmul(Z[n].rearrange("p (h n) -> p h n", n=P), IDB[:, :], mask,
                              start=True, stop=False, skip_group_check=True)
                    last = pe.matmul(Z[n], TQT[:, b * P:(b + 1) * P], TKM[b % 2][:, n * TOK:(n + 1) * TOK],
                                     start=False, stop=True, skip_group_check=True)
                last.then_inc(t_sc.sem, 1)

            def t_turn_p(g, b):
                pe.wait_ge(t_ex.sem, t_ex.at(2, g, b + 1))
                if due(t_pe.before(2, g) + b):
                    pe.wait_ge(t_pe.sem, t_pe.before(2, g) + b)
                for h in range(HEADS):
                    last = pe.transpose(QQ[:, h * P:(h + 1) * P], TE[:, h * P:(h + 1) * P], IDF[:, :])
                last.then_inc(t_tp.sem, 1)

            def t_mix(g, b):
                pe.wait_ge(t_pe.sem, t_pe.at(2, g, b + 1))
                if b == 0:
                    pe.wait_ge(t_ve.sem, t_ve.at(2, g))
                if due(t_cx.before(2, g) + 2 * b):
                    pe.wait_ge(t_cx.sem, t_cx.before(2, g) + 2 * b)
                for h in range(HEADS):
                    at = (b % 2) * 256 + h * (HD + 1)
                    last = pe.matmul(PC[:, at:at + HD + 1], TPT[:, h * P:(h + 1) * P],
                                     TVE[:, span((g % 2) * 4 * VE_ROW + b * VE_ROW + h * (HD + 1), HD + 1)],
                                     start=True, stop=True)
                last.then_inc(t_pv.sem, 1)

            def t_turn_c(g, b):
                pe.wait_ge(t_cx.sem, t_cx.at(2, g))
                pe.wait_ge(t_ve.sem, t_ve.at(2, g + 1 if not (isinstance(g, int) and g == GROUPS - 1) else g))
                turn(PB, TC).then_inc(t_ct.sem, 1)

            def t_out(g, b):
                pe.wait_ge(t_cv.sem, t_cv.at(2, g))
                for n in range(PER_GROUP):
                    last = pe.matmul(PB[:, n * P:(n + 1) * P], TT[:, n * P:(n + 1) * P], mat("l2_wo"),
                                     start=True, stop=True)
                last.then_inc(t_wo.sem, 1)

            def t_turn_n(g, b):
                pe.wait_ge(t_n1.sem, t_n1.at(2, g))
                pe.wait_ge(t_qt.sem, t_qt.at(2, g + 2 if not (isinstance(g, int) and g >= GROUPS - 2) else GROUPS - 1))
                turn(Y[1], TN1).then_inc(t_t1.sem, 1)

            def t_mlp1(g, half_):
                pe.wait_ge(t_nt.sem, t_nt.at(2, g))
                if half_ == 0:
                    if due(t_x.before(2, g)):
                        pe.wait_ge(t_x.sem, t_x.before(2, g))
                for k in (2 * half_, 2 * half_ + 1):
                    if half_:
                        pe.wait_ge(t_mh.sem, t_mh.at(2, g, k - 1))
                    pe.matmul(Y[k % 2], mat("l2_w1", k * P, P), TNT, start=True, stop=True)\
                        .then_inc(t_m1.sem, 1)

            def t_mlp2(g, b):
                pe.wait_ge(t_mh.sem, t_mh.at(2, g))
                pe.wait_ge(t_kt.sem, t_kt.at(2, g + 3 if not (isinstance(g, int) and g >= GROUPS - 3) else GROUPS - 1))
                for n in range(PER_GROUP):
                    for k in range(4):
                        last = pe.matmul(Y[0][:, n * P:(n + 1) * P], H[:, k * TOK + n * P:k * TOK + (n + 1) * P],
                                         mat("l2_w2", k * P, P), start=(k == 0), stop=(k == 3))
                last.then_inc(t_m2.sem, 1)

            def begin():
                pe.wait_ge(consts, N_CONSTS)
                pe.wait_ge(small_in, 48)
                for n, (w, a) in enumerate((("l0_w", "l0_a"), ("l3_wT", "l3_a"))):
                    for side in range(2):
                        last = pe.matmul(PA[:, (2 * n + side) * P:(2 * n + side + 1) * P], mat(w),
                                         col(a, side).to_broadcast([P, P]), start=True, stop=True)
                last.then_inc(v_mm, 1)
                pe.wait_ge(v_done, 1)

            def ahead(layer):
                if layer == 0:
                    pe.wait_ge(w2_in, 48)
                    pe.wait_ge(w_split, 4)
                else:
                    pe.wait_ge(w_split, 6)
                    pe.wait_ge(t_x.sem, t_x.at(2, GROUPS - 1))
                for job in range(AHEAD[layer]):
                    up(layer, 0, job)

            Walk(pe, slot, tail, dict(t_turn=t_turn, t_project=t_project, t_scores=t_scores,
                                      t_turn_p=t_turn_p, t_mix=t_mix, t_turn_c=t_turn_c, t_out=t_out,
                                      t_turn_n=t_turn_n, t_mlp1=t_mlp1, t_mlp2=t_mlp2,
                                      p_turn2=p_turn2, w2_bias=w2_bias, p_turn=p_turn,
                                      p_router=p_router, p_logits=p_logits,
                                      p_gates=p_gates, g_turn=g_turn, g_scores=g_scores,
                                      g_turn_p=g_turn_p, g_mix=g_mix,
                                      g_rel0=lambda la, g: relations(la, g, 0),
                                      g_rel1=lambda la, g: relations(la, g, 1)), begin, ahead).run()

        @block.scalar
        def _(act):
            def hidden_act(layer, g, job):
                if not follows(layer, g) and job >= JOBS[layer]:
                    return
                layer, g, job = job_at(layer, g, job)
                act.wait_ge(z_full.sem, z_full.at(layer, g, job + 1))
                if layer == 1:
                    bias = col("l1_b1", L1_FIRST.index(job)) if job in L1_FIRST else \
                        col("l1_b2", L1_SECOND.index(job))
                elif layer == 2:
                    bias = LNB1[:, job:job + 1]
                else:
                    bias = col(f"l{layer}_b1", job)
                act.activation(H[:, (job % HB) * TOK:(job % HB + 1) * TOK], Z[job % 2][:, :],
                               ACT.Gelu if layer in (0, 2) else ACT.Relu, bias=bias).then_inc(h_done.sem, 1)
                if layer > 1:
                    act.activation(HH[:, (job % HB) * TOK:(job % HB + 1) * TOK], Z[job % 2][:, :],
                                   ACT.Gelu if layer == 2 else ACT.Relu, bias=bias).then_inc(h_hi.sem, 1)

            def slot(layer, g, e):
                if e < 0:
                    hidden_act(layer, g, 2)
                    return
                nb = BLOCKS[layer]

                def gate():
                    act.wait_ge(g_full.sem, g_full.at(layer, g, e + 1))
                    if due(comb.before(layer, g) + e - 1):
                        act.wait_ge(comb.sem, comb.before(layer, g) + e - 1)
                    act.activation(GS[:, (e % 2) * TOK:(e % 2 + 1) * TOK], GB[:, :], ACT.Copy)\
                        .then_inc(gs_done.sem, 1)

                if layer == 1:
                    gate()
                    hidden_act(layer, g, 2 * e + 3)
                    hidden_act(layer, g, 2 * e + 4)
                    return
                for k in range(nb):
                    if k == 0 and layer == 0:
                        gate()
                    hidden_act(layer, g, e * nb + k + AHEAD[layer])

            def p_turn(layer, g):
                act.wait_ge(p_tr.sem, p_tr.at(layer, g, 1))
                act.activation(pt(layer, g)[:, :], PC[:, :], ACT.Copy).then_inc(p_ev.sem, 1)

            def p_router(layer, g):
                act.wait_ge(p_r1.sem, p_r1.at(layer, g))
                act.activation(PX[0:64, :], PC[0:64, :], ACT.Relu,
                               bias=COLW[0:64, COL_AT["l1_rb1"][0]:COL_AT["l1_rb1"][0] + 1]).then_inc(p_rh.sem, 1)

            def p_weigh(layer, g):
                if layer == 1:
                    act.wait_ge(p_dv.sem, p_dv.at(layer, g, ROUTED[1]))
                    act.activation(RT[:, EXPS], RT[:, EXPS], ACT.Exp).then_inc(p_ex.sem, 1)
                    act.wait_ge(p_dv.sem, p_dv.at(layer, g, WEIGHED))
                    act.activation(RV[:, 8:12], RV[:, 8:12], ACT.Exp).then_inc(p_ex.sem, 1)
                elif layer > 1:
                    act.wait_ge(p_dv.sem, p_dv.at(layer, g, ROUTED[layer]))
                    act.activation(RV[:, 8:12], RV[:, 8:12], ACT.Exp).then_inc(p_ex.sem, 1)

            def p_gates(layer, g):
                act.wait_ge(p_gt.sem, p_gt.at(layer, g))
                act.activation(half(GT, g, 24), PC[0:24, 0:TOK // 2].bitcast(BF16), ACT.Copy)\
                    .then_inc(p_ge.sem, 1)

            def g_turn(layer, g):
                act.wait_ge(g_tr.sem, g_tr.at(layer, g))
                act.activation(GXT, PA[:, :], ACT.Copy).then_inc(g_ev.sem, 1)

            def g_scores(layer, g):
                act.wait_ge(g_sc.sem, g_sc.at(layer, g))
                if layer == 0:
                    act.activation(GZ, PA[:, :], ACT.Copy).then_inc(g_se.sem, 1)
                act.activation(GH, PB[:, :], ACT.Copy).then_inc(g_se.sem, 1)

            def g_exp(layer, g):
                act.wait_ge(g_ce.sem, g_ce.at(layer, g))
                act.activation(GP, GE, ACT.Exp).then_inc(g_ex.sem, 1)

            def g_turn_p(layer, g):
                act.wait_ge(g_pt.sem, g_pt.at(layer, g))
                act.activation(GPT, PA[:, :], ACT.Copy).then_inc(g_pe.sem, 1)

            def relations(layer, g, pair):
                act.wait_ge(g_tr.sem, g_tr.at(layer, g, pair + 1))
                for b, bank in ((2 * pair, PA), (2 * pair + 1, PB)):
                    act.activation(GHT[:, b * RELATIONS * P:(b + 1) * RELATIONS * P], bank[:, :], ACT.Copy)\
                        .then_inc(g_ev.sem, 1)

            def g_add(layer, g):
                if layer == 3:
                    act.wait_ge(g_ad.sem, g_ad.at(layer, g, 2))
                    act.activation(GE, GZ, ACT.Exp).then_inc(g_el.sem, 1)

            def p_turn2(layer, g):
                act.wait_ge(p_tr.sem, p_tr.at(layer, g, 2))
                act.wait_ge(p_lg.sem, p_lg.at(layer, g))
                act.activation(pt(layer, g)[:, :], PC[:, :], ACT.Copy).then_inc(p_ev.sem, 1)

            def t_turn(g, b):
                act.wait_ge(t_tr.sem, t_tr.at(2, g))
                act.activation(TT, Y[0], ACT.Copy).then_inc(t_ut.sem, 1)

            def t_project(g, b):
                act.wait_ge(t_qkv.sem, t_qkv.at(2, g, 1))
                act.activation(TKT_RING[:, span((g % 2) * TOK, TOK)], Y[0], ACT.Identity,
                               bias=col("l2_bk")).then_inc(t_kt.sem, 1)

            def t_queries(g, b):
                act.wait_ge(t_qkv.sem, t_qkv.at(2, g, 2))
                if due(t_sc.before(2, g)):
                    act.wait_ge(t_sc.sem, t_sc.before(2, g))
                act.activation(TQT, Y[1], ACT.Identity, bias=BQ4[:, :], scale=HD ** -0.5)\
                    .then_inc(t_qt.sem, 1)

            def t_scores(g, b):
                act.wait_ge(t_ce.sem, t_ce.at(2, g, 2 * b + 2))
                act.activation(TE, TE, ACT.Exp).then_inc(t_ex.sem, 1)

            def t_turn_p(g, b):
                act.wait_ge(t_tp.sem, t_tp.at(2, g, b + 1))
                act.activation(TPT, QQ[:, :], ACT.Copy).then_inc(t_pe.sem, 1)

            def t_turn_c(g, b):
                act.wait_ge(t_ct.sem, t_ct.at(2, g))
                act.activation(TT, PB[:, :], ACT.Copy).then_inc(t_cv.sem, 1)

            def t_turn_n(g, b):
                act.wait_ge(t_t1.sem, t_t1.at(2, g))
                act.activation(TNT, Y[1], ACT.Copy).then_inc(t_nt.sem, 1)

            def t_mlp1(g, half_):
                for k in (2 * half_, 2 * half_ + 1):
                    act.wait_ge(t_m1.sem, t_m1.at(2, g, k + 1))
                    act.activation(H[:, k * TOK:(k + 1) * TOK], Y[k % 2], ACT.Relu,
                                   bias=col("l2_mb1", k)).then_inc(t_mh.sem, 1)

            def begin():
                act.dma_start(MATW[:, :], mats).then_inc(small_in, 16)
                act.dma_start(COLW[:, :], cols).then_inc(small_in, 16)
                act.dma_start(ROWW[:, :], rows.partition_broadcast(P)).then_inc(small_in, 16)
                act.wait_ge(v_mm, 1)
                act.activation(V[:, :], PA[:, :], ACT.Copy).then_inc(v_done, 1)
                act.wait_ge(consts, N_CONSTS)

            def ahead(layer):
                for job in range(AHEAD[layer]):
                    hidden_act(layer, 0, job)

            Walk(act, slot, lambda layer, g: None,
                 dict(t_turn=t_turn, t_project=t_project, t_queries=t_queries, t_scores=t_scores,
                      t_turn_p=t_turn_p, t_turn_c=t_turn_c, t_turn_n=t_turn_n, t_mlp1=t_mlp1,
                      p_turn2=p_turn2, p_turn=p_turn, p_router=p_router, p_weigh=p_weigh,
                      p_gates=p_gates, g_turn=g_turn,
                      g_scores=g_scores, g_exp=g_exp, g_turn_p=g_turn_p, g_add=g_add,
                      g_rel0=lambda la, g: relations(la, g, 0),
                      g_rel1=lambda la, g: relations(la, g, 1)), begin, ahead).run()

        @block.vector
        def _(dve):
            def norm_stats(ch, src, st, mv, rs):
                for b in range(PER_GROUP):
                    dve.bn_stats(st[:, 6 * b:6 * b + 6], src(b)).then_inc(ch.sem, ch.one())
                dve.wait_ge(ch.sem, ch.value())
                dve.memset(rs[:, :], EPS)
                for b in range(PER_GROUP):
                    dve.bn_aggr(mv[:, 2 * b:2 * b + 2], st[:, 6 * b:6 * b + 6]).then_inc(ch.sem, ch.one())
                dve.wait_ge(ch.sem, ch.value())
                var = graphs(mv[:, :], 2)[:, :, 1]
                dve.tensor_tensor(rs[:, :], var, rs[:, :], ALU.add).then_inc(ch.sem, ch.one())

            def norm_apply(ch, src, dst, mv, rs):
                for b in range(PER_GROUP):
                    dve.tensor_scalar(dst[:, b * P:(b + 1) * P], src(b), mv[:, 2 * b:2 * b + 1],
                                             rs[:, b:b + 1], ALU.subtract, ALU.mult).then_inc(ch.sem, ch.one())
                dve.wait_ge(ch.sem, ch.value())

            def x_graph(g):
                return lambda b: X[:, span(g * TOK + b * P, P)]

            def hidden_lo(layer, g, job):
                if not follows(layer, g) and job >= JOBS[layer]:
                    return
                layer, g, job = job_at(layer, g, job)
                dve.wait_ge(h_hi.sem, h_hi.at(layer, g, job + 1))
                at = (job % HB) * TOK
                dve.tensor_tensor(HL[:, at:at + TOK], H[:, at:at + TOK], HH[:, at:at + TOK].bitcast(F32),
                                  ALU.subtract).then_inc(h_lo_first.sem, 1)

            def slot(layer, g, e):
                if e < 0:
                    return
                if layer > 1:
                    dve.wait_ge(g_full.sem, g_full.at(layer, g, e + 1))
                    dve.wait_ge(comb.sem, comb.before(layer, g) + e - 1)
                    dve.tensor_copy(GS[:, (e % 2) * TOK:(e % 2 + 1) * TOK], GB[:, :]).then_inc(gs_done.sem, 1)
                    hidden_lo(layer, g, 4 * e + 4)
                dve.wait_ge(y_full.sem, y_full.at(layer, g, e + 1))
                dve.wait_ge(gs_done.sem, gs_done.at(layer, g, e + 1))
                if e == 0:
                    if layer or not (isinstance(g, int) and g == 0):
                        if due(tail_tr.before(layer, g)):
                            dve.wait_ge(tail_tr.sem, tail_tr.before(layer, g))
                    dst = ACC[:, :]
                else:
                    if due(acc_done.before(layer, g) + max(e - 2, 0)):
                        dve.wait_ge(acc_done.sem, acc_done.before(layer, g) + max(e - 2, 0))
                    dst = T[:, (e % 2) * TOK:(e % 2 + 1) * TOK]
                b2 = col("l1_b3" if layer == 1 else f"l{layer}_b2", e)
                dve.scalar_tensor_tensor(dst, Y[e % 2][:, :], b2, GS[:, (e % 2) * TOK:(e % 2 + 1) * TOK],
                                         ALU.add, ALU.mult).then_inc(comb.sem, 1)

            def tail(layer, g):
                dve.wait_ge(tail_tr.sem, tail_tr.at(layer, g))
                dve.tensor_tensor(x_at(g), PC[:, :], x_at(g), ALU.add).then_inc(tail_x.sem, 1)

            def p_norm(layer, g):
                if layer == 2:
                    dve.wait_ge(t_x.sem, t_x.at(layer, g))
                else:
                    dve.wait_ge(g_ad.sem, g_ad.at(layer, g))
                if due(p_lg.before(layer, g)):
                    dve.wait_ge(p_lg.sem, p_lg.before(layer, g))
                norm_stats(Count(p_ln, layer, g), x_graph(g), ST, MV, RS)

            def p_apply(layer, g):
                dve.wait_ge(p_rs.sem, p_rs.at(layer, g, 1))
                if early(layer, g):
                    dve.wait_ge(t_km.sem, t_km.at(2, GROUPS - 1))
                norm_apply(Count(p_ln, layer, g, 9), x_graph(g), px(layer, g), MV, RS)

            def p_norm2(layer, g):
                norm_stats(Count(p_ln, layer, g, 13), px_graph(g), ST, MV, RS)

            def p_apply2(layer, g):
                dve.wait_ge(p_rs.sem, p_rs.at(layer, g, 2))
                norm_apply(Count(p_ln, layer, g, 22), px_graph(g), px2(layer, g), MV, RS)

            def px_graph(g):
                return lambda b: px(2, g)[:, b * P:(b + 1) * P]

            def p_split(layer, g):
                dve.wait_ge(p_ev.sem, p_ev.at(layer, g))
                ch = Count(p_sp, layer, g)
                dve.tensor_copy(half(XH, g), pt(layer, g)[:, :]).then_inc(p_sp.sem, ch.one())
                dve.wait_ge(p_sp.sem, ch.value())
                dve.tensor_tensor(half(XL, g), pt(layer, g)[:, :], half(XH, g).bitcast(F32), ALU.subtract)\
                    .then_inc(p_sp.sem, ch.one())
                ch.full()

            def rt(i):
                return RT[:, 32 * i:32 * i + 32].rearrange("p (b e) -> p b e", e=8)

            def rv(i):
                return RV[:, 4 * i:4 * i + 4]

            def wide(v):
                return v.unsqueeze(2).to_broadcast([P, PER_GROUP, 8])

            def p_route(layer, g):
                dve.wait_ge(p_lg.sem, p_lg.at(layer, g))
                ch = Count(p_dv, layer, g)
                n = EXPERTS[layer]
                iota = IOTA[:, :].unsqueeze(1).to_broadcast([P, PER_GROUP, 8])
                lg, eq, key, one, two, rest, gate = (rt(i) for i in range(7))
                m1, m2, at = rv(0), rv(1), rv(3)
                if layer == 1:
                    dve.memset(lg[:, :, n:8], BARRED).then_inc(p_dv.sem, ch.one())
                dve.tensor_tensor(lg[:, :, 0:n], graphs(PC[:, 0:32], 8)[:, :, 0:n],
                                          row(f"l{layer}_bg").unsqueeze(1).to_broadcast([P, PER_GROUP, n]),
                                          ALU.add).then_inc(p_dv.sem, ch.one())
                dve.wait_ge(p_dv.sem, ch.value())
                for src, m, hot in ((lg, m1, one), (rest, m2, two)):
                    dve.tensor_reduce(m, src, AX, ALU.max).then_inc(p_dv.sem, ch.one())
                    dve.wait_ge(p_dv.sem, ch.value())
                    dve.tensor_tensor(eq, src, wide(m), ALU.is_equal).then_inc(p_dv.sem, ch.one())
                    dve.wait_ge(p_dv.sem, ch.value())
                    dve.scalar_tensor_tensor(key, eq, -64.0, iota, ALU.mult, ALU.add).then_inc(p_dv.sem, ch.one())
                    dve.wait_ge(p_dv.sem, ch.value())
                    dve.tensor_reduce(at, key, AX, ALU.min).then_inc(p_dv.sem, ch.one())
                    dve.wait_ge(p_dv.sem, ch.value())
                    dve.tensor_tensor(hot, key, wide(at), ALU.is_equal).then_inc(p_dv.sem, ch.one())
                    dve.wait_ge(p_dv.sem, ch.value())
                    if hot is one:
                        dve.scalar_tensor_tensor(rest, one, 2 * BARRED, lg, ALU.mult, ALU.add)\
                            .then_inc(p_dv.sem, ch.one())
                        dve.wait_ge(p_dv.sem, ch.value())
                if layer == 1:
                    dve.tensor_tensor(RT[:, EXPS][:, 0:32].rearrange("p (b e) -> p b e", e=8), lg, wide(m1),
                                      ALU.subtract).then_inc(p_dv.sem, ch.one())
                    dve.tensor_tensor(RT[:, EXPS][:, 32:36], m2, m1, ALU.subtract).then_inc(p_dv.sem, ch.one())
                elif layer:
                    dve.tensor_tensor(rv(2), m2, m1, ALU.subtract).then_inc(p_dv.sem, ch.one())
                dve.wait_ge(p_dv.sem, ch.value())
                assert ch.n == ROUTED[layer], ch.n

            def p_weigh(layer, g):
                ch = Count(p_dv, layer, g, ROUTED[layer])
                one, two, gate = rt(3), rt(4), rt(6)
                m_ex, w1, w2, t1 = rv(2), rv(4), rv(5), rv(6)
                if layer == 0:
                    dve.tensor_tensor(gate, one, two, ALU.add).then_inc(p_dv.sem, ch.one())
                    dve.wait_ge(p_dv.sem, ch.value())
                else:
                    if layer == 1:
                        e9 = RT[:, EXPS]
                        dve.wait_ge(p_ex.sem, p_ex.at(layer, g, 1))
                        dve.tensor_reduce(t1, e9[:, 0:32].rearrange("p (b e) -> p b e", e=8), AX, ALU.add)\
                            .then_inc(p_dv.sem, ch.one())
                        dve.wait_ge(p_dv.sem, ch.value())
                        dve.reciprocal(t1, t1).then_inc(p_dv.sem, ch.one())
                        dve.wait_ge(p_dv.sem, ch.value())
                        dve.scalar_tensor_tensor(m_ex, e9[:, 32:36], -1.0, t1, ALU.add, ALU.mult)\
                            .then_inc(p_dv.sem, ch.one())
                        assert ch.n == WEIGHED, ch.n
                    dve.wait_ge(p_ex.sem, p_ex.at(layer, g))
                    dve.tensor_scalar(w1, m_ex, 1.0, None, ALU.add).then_inc(p_dv.sem, ch.one())
                    dve.wait_ge(p_dv.sem, ch.value())
                    dve.reciprocal(w1, w1).then_inc(p_dv.sem, ch.one())
                    dve.wait_ge(p_dv.sem, ch.value())
                    dve.tensor_tensor(w2, m_ex, w1, ALU.mult).then_inc(p_dv.sem, ch.one())
                    dve.wait_ge(p_dv.sem, ch.value())
                    dve.tensor_tensor(one, one, wide(w1), ALU.mult).then_inc(p_dv.sem, ch.one())
                    dve.tensor_tensor(two, two, wide(w2), ALU.mult).then_inc(p_dv.sem, ch.one())
                    dve.wait_ge(p_dv.sem, ch.value())
                    dve.tensor_tensor(gate, one, two, ALU.add).then_inc(p_dv.sem, ch.one())
                    dve.wait_ge(p_dv.sem, ch.value())
                g3 = graphs(GB3[:, :], 24)
                dve.tensor_copy(g3[:, :, 0:8], gate).then_inc(p_dv.sem, ch.one())
                dve.wait_ge(p_dv.sem, ch.value())
                dve.tensor_tensor(gate, gate, g3[:, :, 0:8], ALU.subtract).then_inc(p_dv.sem, ch.one())
                dve.wait_ge(p_dv.sem, ch.value())
                dve.tensor_copy(g3[:, :, 8:16], gate).then_inc(p_dv.sem, ch.one())
                dve.wait_ge(p_dv.sem, ch.value())
                dve.tensor_tensor(g3[:, :, 16:24], gate, g3[:, :, 8:16], ALU.subtract).then_inc(p_dv.sem, ch.one())
                dve.wait_ge(p_dv.sem, ch.value())
                ch.full()

            def g_norm(layer, g):
                if layer == 0 and isinstance(g, int) and g == 2:
                    dve.wait_ge(x_rest, 16)
                if layer:
                    dve.wait_ge(tail_x.sem, tail_x.at(layer - 1, g))
                norm_stats(Count(g_ln, layer, g), x_graph(g), GST, GMV, GRS)
                dve.wait_ge(adj_in.sem, adj_in.at(layer, g))
                pen = Count(g_pen, layer, g)
                a = half(ADJ, g)
                if layer == 1:
                    gm = GM.rearrange("p (b r n) -> p b r n", r=RELATIONS, n=P)
                    for r in range(RELATIONS):
                        dve.tensor_scalar(gm[:, :, r, :], graphs(a), float(r + 1), None, ALU.is_equal)\
                            .then_inc(g_pen.sem, pen.one())
                else:
                    dve.tensor_scalar(PEN[:, :], a, 0.0, MASKED,
                                              ALU.is_equal if layer == 0 else ALU.is_le, ALU.mult)\
                                                  .then_inc(g_pen.sem, pen.one())
                pen.full()

            def g_apply(layer, g):
                dve.wait_ge(g_rs.sem, g_rs.at(layer, g))
                norm_apply(Count(g_ln, layer, g, 9), x_graph(g), GXN, GMV, GRS)
                if layer == 0 and isinstance(g, int) and g == 0:
                    dve.wait_ge(w1_in, 32)
                    split_weights(H[:, :], W[:, 0:2048], W[:, 2048:4096], w_split, 0)
                    split_weights(T[:, 0:768], W[:, 8192:8960], W[:, 8960:9728], w_split, 2)

            def g_center(layer, g):
                dve.wait_ge(g_se.sem, g_se.at(layer, g))
                ch = Count(g_ce, layer, g)
                mx = GR[:, 0:4]
                if layer == 0:
                    dve.scalar_tensor_tensor(GE, GZ, 0.2, PA[:, :], ALU.mult, ALU.max).then_inc(g_ce.sem, ch.one())
                    dve.wait_ge(g_ce.sem, ch.value())
                    z = GE
                else:
                    z = PA[:, :]
                dve.tensor_reduce(mx, graphs(z), AX, ALU.max).then_inc(g_ce.sem, ch.one())
                dve.wait_ge(g_ce.sem, ch.value())
                dve.tensor_tensor(graphs(GE), graphs(z), mx.unsqueeze(2).to_broadcast([P, PER_GROUP, P]),
                                         ALU.subtract).then_inc(g_ce.sem, ch.one())
                ch.full()

            def g_turn_p(layer, g):
                dve.wait_ge(g_ex.sem, g_ex.at(layer, g))
                ch = Count(g_su, layer, g)
                dve.tensor_reduce(GR[:, 4:8], graphs(GP), AX, ALU.add).then_inc(g_su.sem, ch.one())
                dve.wait_ge(g_su.sem, ch.value())
                dve.reciprocal(GR[:, 8:12], GR[:, 4:8]).then_inc(g_su.sem, ch.one())
                dve.wait_ge(g_su.sem, ch.value())
                ch.full()

            def g_add(layer, g):
                dve.wait_ge(g_mx.sem, g_mx.at(layer, g))
                ch = Count(g_ad, layer, g)
                if layer == 1:
                    bias = row("l1_bias").unsqueeze(1).to_broadcast([P, PER_GROUP, P])
                    dve.tensor_tensor(graphs(GXN), graphs(PA[:, :]), bias, ALU.add).then_inc(g_ad.sem, ch.one())
                    dve.wait_ge(g_ad.sem, ch.value())
                    dve.tensor_tensor(x_at(g), GXN, x_at(g), ALU.add).then_inc(g_ad.sem, ch.one())
                else:
                    norm_ = GR[:, 8:12].unsqueeze(2).to_broadcast([P, PER_GROUP, P])
                    dve.tensor_tensor(graphs(GP), graphs(PB[:, :]), norm_, ALU.mult).then_inc(g_ad.sem, ch.one())
                    dve.wait_ge(g_ad.sem, ch.value())
                    if layer == 0:
                        dve.tensor_tensor(x_at(g), GP, x_at(g), ALU.add).then_inc(g_ad.sem, ch.one())
                    else:
                        dve.tensor_scalar(GZ, GP, 0.0, None, ALU.min).then_inc(g_ad.sem, ch.one())
                        dve.wait_ge(g_el.sem, g_el.at(layer, g))
                        dve.scalar_tensor_tensor(GP, GP, 0.0, GE, ALU.max, ALU.add).then_inc(g_ad.sem, ch.one())
                        dve.wait_ge(g_ad.sem, ch.value())
                        dve.scalar_tensor_tensor(x_at(g), GP, -1.0, x_at(g), ALU.add, ALU.add)\
                            .then_inc(g_ad.sem, ch.one())
                ch.full()

            def w2_split(layer, part):
                if part == 0:
                    dve.wait_ge(w_bias, 1)
                    dve.tensor_tensor(LNB1[:, :], PA[:, 0:32], COLW[:, COL_AT["l2_b1"][0]:COL_AT["l2_b1"][0] + 32],
                                      ALU.add).then_inc(l2_consts, 1)
                    dve.tensor_scalar(BQ4[:, :], col("l2_bq"), HD ** -0.5, None, ALU.mult).then_inc(l2_consts, 1)
                    for e in range(8):
                        w = SCR[:, e * 4 * P:(e + 1) * 4 * P]
                        dve.tensor_scalar(w, w, col("l2_lng", e), None, ALU.mult).then_inc(l2_consts, 1)
                elif part == 1:
                    dve.wait_ge(l2_consts, 10)
                    split_weights(SCR[:, 0:4096], W[:, 0:4096], W[:, 4096:8192], w_split, 4)

            def w3_split(layer, e):
                stage, at = W3_STAGE[e % 2], e * 4 * P
                dve.wait_ge(l3_in[e % 2], 32 * (e // 2 + 1))
                split_weights(stage[:, 0:4 * P], W[:, at:at + 4 * P], W[:, 4096 + at:4096 + at + 4 * P],
                              l3_split, 4 * e)
                split_weights(stage[:, 4 * P:8 * P], W[:, W2_HI + at:W2_HI + at + 4 * P],
                              W[:, W2_LO + at:W2_LO + at + 4 * P], l3_split, 4 * e + 2)

            def t_norm(g, b):
                dve.wait_ge(tail_x.sem, tail_x.at(1, g))
                if isinstance(g, int) and g == 0:
                    dve.wait_ge(w_split, 6)
                norm_stats(Count(t_ln, 2, g), x_graph(g), GST, GMV, GRS)

            def t_apply(g, b):
                dve.wait_ge(t_rw[0].sem, t_rw[0].at(2, g))
                norm_apply(Count(t_ln, 2, g, 9), x_graph(g), TU, GMV, GRS)
                ch = Count(t_ln, 2, g, 13)
                dve.tensor_copy(TU_RING[:, span((g % 4) * TOK, TOK)], TU).then_inc(t_ln.sem, ch.one())
                ch.full()

            def t_mask(g, b):
                if isinstance(g, int) and g == 0:
                    ones = TVE.rearrange("p (h n) -> p h n", n=HD + 1)[:, :, HD:HD + 1]
                    dve.memset(ones, 1.0).then_inc(l2_consts, 1)
                dve.wait_ge(t_qkv.sem, t_qkv.at(2, g))
                ve = TVE[:, span((g % 2) * 4 * VE_ROW, 4 * VE_ROW)].rearrange("p (b h n) -> p b h n", b=4, n=HD + 1)
                dve.tensor_tensor(ve[:, :, :, 0:HD], PB[:, :].rearrange("p (b h n) -> p b h n", b=4, n=HD),
                                  row("l2_bv").rearrange("p (h n) -> p h n", n=HD).unsqueeze(1)
                                  .to_broadcast([P, 4, HEADS, HD]), ALU.add).then_inc(t_ve.sem, 1)
                dve.wait_ge(adj_in.sem, adj_in.at(2, g))
                if due(t_sc.before(2, g)):
                    dve.wait_ge(t_sc.sem, t_sc.before(2, g))
                ch = Count(t_pen, 2, g)
                dve.tensor_tensor(TM, ADJ[:, 0:TOK], ADJ[:, TOK:2 * TOK], ALU.max).then_inc(t_pen.sem, ch.one())
                dve.wait_ge(t_pen.sem, ch.value())
                dve.scalar_tensor_tensor(graphs(PEN[:, :]), graphs(TM), 0.0,
                                                NEB[:, :].unsqueeze(1).to_broadcast([P, PER_GROUP, P]),
                                                ALU.is_le, ALU.mult).then_inc(t_pen.sem, ch.one())
                ch.full()

            def t_scores(g, b):
                dve.wait_ge(t_sc.sem, t_sc.at(2, g, b + 1))
                ch = Count(t_ce, 2, g, 2 * b)
                s = ZZ[:, :].rearrange("p (h n) -> p h n", n=P)
                mx = RV[:, 16:24]
                dve.tensor_reduce(mx, s, AX, ALU.max).then_inc(t_ce.sem, ch.one())
                dve.wait_ge(t_ce.sem, ch.value())
                dve.tensor_tensor(TE.rearrange("p (h n) -> p h n", n=P), s,
                                         mx.unsqueeze(2).to_broadcast([P, HEADS, P]), ALU.subtract)\
                                             .then_inc(t_ce.sem, ch.one())

            def t_mix(g, b):
                dve.wait_ge(t_pv.sem, t_pv.at(2, g, b + 1))
                ch = Count(t_cx, 2, g, 2 * b)
                o = PC[:, (b % 2) * 256:(b % 2) * 256 + VE_ROW].rearrange("p (h n) -> p h n", n=HD + 1)
                dve.reciprocal(TRC.unsqueeze(2), o[:, :, HD:HD + 1]).then_inc(t_cx.sem, ch.one())
                dve.wait_ge(t_cx.sem, ch.value())
                dve.tensor_tensor(TC[:, b * P:(b + 1) * P].rearrange("p (h n) -> p h n", n=HD),
                                         o[:, :, 0:HD], TRC.unsqueeze(2).to_broadcast([P, HEADS, HD]), ALU.mult)\
                                             .then_inc(t_cx.sem, ch.one())

            def spread(name):
                return row(name).unsqueeze(1).to_broadcast([P, PER_GROUP, P])

            def in_graph(t):
                return lambda b: t[:, b * P:(b + 1) * P]

            def t_out(g, b):
                dve.wait_ge(t_wo.sem, t_wo.at(2, g))
                ch = Count(t_n1, 2, g)
                dve.tensor_tensor(graphs(TN1), graphs(PB[:, :]), spread("l2_bo"), ALU.add)\
                    .then_inc(t_n1.sem, ch.one())
                dve.wait_ge(t_n1.sem, ch.value())
                dve.tensor_tensor(TN1, TN1, TU_RING[:, span((g % 4) * TOK, TOK)], ALU.add)\
                    .then_inc(t_n1.sem, ch.one())
                dve.wait_ge(t_n1.sem, ch.value())
                norm_stats(ch, in_graph(TN1), ST, MV, RS)

            def t_norm1(g, b):
                dve.wait_ge(t_rw[1].sem, t_rw[1].at(2, g))
                ch = Count(t_n1, 2, g, 11)
                norm_apply(ch, in_graph(TN1), TN1, MV, RS)
                dve.tensor_tensor(graphs(TN1), graphs(TN1), spread("l2_g1"), ALU.mult).then_inc(t_n1.sem, ch.one())
                dve.wait_ge(t_n1.sem, ch.value())
                dve.tensor_tensor(graphs(TN1), graphs(TN1), spread("l2_c1"), ALU.add).then_inc(t_n1.sem, ch.one())
                dve.wait_ge(t_n1.sem, ch.value())
                dve.tensor_tensor(graphs(TNB_RING[:, span((g % 2) * TOK, TOK)]), graphs(TN1),
                                         spread("l2_mb2"), ALU.add).then_inc(t_n1.sem, ch.one())
                ch.full()

            def t_mlp2(g, b):
                dve.wait_ge(t_m2.sem, t_m2.at(2, g))
                ch = Count(t_x, 2, g)
                dve.tensor_tensor(TR2, Y[0], TNB_RING[:, span((g % 2) * TOK, TOK)], ALU.add)\
                    .then_inc(t_x.sem, ch.one())
                dve.wait_ge(t_x.sem, ch.value())
                norm_stats(ch, in_graph(TR2), ST2, MV2, RV[:, 12:16])

            def t_norm2(g, b):
                dve.wait_ge(t_rw[2].sem, t_rw[2].at(2, g))
                ch = Count(t_x, 2, g, 10)
                norm_apply(ch, in_graph(TR2), TR2, MV2, RV[:, 12:16])
                dve.tensor_tensor(graphs(TR2), graphs(TR2), spread("l2_g2"), ALU.mult).then_inc(t_x.sem, ch.one())
                dve.wait_ge(t_x.sem, ch.value())
                dve.tensor_tensor(graphs(TR2), graphs(TR2), spread("l2_c2"), ALU.add).then_inc(t_x.sem, ch.one())
                dve.wait_ge(t_x.sem, ch.value())
                dve.tensor_tensor(x_at(g), TR2, x_at(g), ALU.add).then_inc(t_x.sem, ch.one())
                dve.wait_ge(t_x.sem, ch.value())
                ch.full()
                if isinstance(g, int) and g == GROUPS - 2:
                    dve.wait_ge(l2_in, 32)
                    split_weights(SCR[:, 0:4096], W[:, W2_HI:W2_HI + 4096], W[:, W2_LO:W2_LO + 4096],
                                  w_split, 6)

            def split_weights(stage, hi, lo, done, count):
                dve.tensor_copy(hi, stage).then_inc(done, 1)
                dve.wait_ge(done, count + 1)
                dve.tensor_tensor(lo, stage, hi.bitcast(F32), ALU.subtract).then_inc(done, 1)

            def begin():
                dve.wait_ge(x_first, 16)
                dve.wait_ge(consts, N_CONSTS)
                dve.wait_ge(small_in, 48)

            def ahead(layer):
                if layer:
                    hidden_lo(layer, 0, 0)

            Walk(dve, slot, tail, dict(w2_split=w2_split, w3_split=w3_split, t_norm=t_norm, t_apply=t_apply,
                                       t_mask=t_mask, t_scores=t_scores, t_mix=t_mix, t_out=t_out,
                                       t_norm1=t_norm1, t_mlp2=t_mlp2, t_norm2=t_norm2,
                                       p_norm=p_norm, p_apply=p_apply, p_norm2=p_norm2, p_apply2=p_apply2,
                                       g_apply=g_apply, p_split=p_split, p_route=p_route, p_weigh=p_weigh, g_norm=g_norm,
                                       g_center=g_center, g_turn_p=g_turn_p, g_add=g_add),
                 begin, ahead).run()


def arrange(inputs):
    a = {k: np.asarray(v) for k, v in inputs.items()}

    def column(v, rows=P):
        m = np.zeros((P, v.size // rows), np.float32)
        m[:rows] = v.reshape(-1, rows).T
        return m

    def tall(w):
        e, k, n = w.shape
        return np.ascontiguousarray(w.reshape(e, k // P, P, n).transpose(2, 0, 1, 3).reshape(P, -1))

    def rows64(w):
        m = np.zeros((P, w.shape[1]), np.float32)
        m[:w.shape[0]] = w
        return m

    wqkv, bqkv = a["L2_gnn_Wqkv"], a["L2_gnn_bqkv"]
    cols = dict(
        l0_b1=column(a["L0_ffn_b1"]), l0_b2=column(a["L0_ffn_b2"]), l0_a=column(a["L0_gnn_a"]),
        l1_rb1=column(a["L1_ffn_router_b1"], 64), l1_b1=column(a["L1_ffn_expert_b1"]),
        l1_b2=column(a["L1_ffn_expert_b2"]), l1_b3=column(a["L1_ffn_expert_b3"]),
        l2_bq=column(bqkv[0:P]), l2_bk=column(bqkv[P:2 * P]), l2_mb1=column(a["L2_gnn_b1"]),
        l2_b1=column(a["L2_ffn_b1"]), l2_b2=column(a["L2_ffn_b2"]), l2_lng=column(a["L2_ffn_ln_g"]),
        l2_lnb=column(a["L2_ffn_ln_b"]), l3_a=column(a["L3_gnn_a"]), l3_b1=column(a["L3_ffn_b1"]),
        l3_b2=column(a["L3_ffn_b2"]))
    rows = dict(
        l0_bg=a["L0_ffn_bg"], l1_bg=a["L1_ffn_router_b2"], l2_bg=a["L2_ffn_br"], l3_bg=a["L3_ffn_bg"],
        l1_bias=a["L1_gnn_bias"], l2_bv=bqkv[2 * P:], l2_bo=a["L2_gnn_bo"], l2_g1=a["L2_gnn_ln1_g"],
        l2_c1=a["L2_gnn_ln1_b"], l2_mb2=a["L2_gnn_b2"], l2_g2=a["L2_gnn_ln2_g"], l2_c2=a["L2_gnn_ln2_b"])
    mats = dict(
        l0_wT=a["L0_gnn_W"].T, l0_w=a["L0_gnn_W"], l0_wg=a["L0_ffn_Wg"],
        l1_w=tall(a["L1_gnn_weight"]), l1_rw1=a["L1_ffn_router_w1"], l1_rw2=rows64(a["L1_ffn_router_w2"]),
        l2_wq=wqkv[0:P].T, l2_wk=wqkv[P:2 * P].T, l2_wv=wqkv[2 * P:].T, l2_wo=a["L2_gnn_Wo"].T,
        l2_w1=a["L2_gnn_W1"].T, l2_w2=tall(a["L2_gnn_W2"].T[None]), l2_wg=a["L2_ffn_Wr"],
        l3_w=a["L3_gnn_W"], l3_wT=a["L3_gnn_W"].T, l3_wg=a["L3_ffn_Wg"].T)

    def pack(table, parts):
        for name, n in table:
            assert parts[name].shape[-1] == n, (name, parts[name].shape)
        return np.ascontiguousarray(np.concatenate([parts[name] for name, _ in table], axis=-1))

    return dict(
        x=a["x"], adj=a["adj"], adjT=np.ascontiguousarray(a["adj"].transpose(0, 2, 1)),
        mats=pack(MATS, mats), cols=pack(COLS, cols), rows=pack(ROWS, rows)[None],
        l0_w1=tall(a["L0_ffn_W1"]), l0_w2=tall(a["L0_ffn_W2"]),
        l1_w1=tall(a["L1_ffn_expert_w1"]), l1_w2=tall(a["L1_ffn_expert_w2"]),
        l1_w3=tall(a["L1_ffn_expert_w3"]),
        l2_w1=tall(a["L2_ffn_W1"]), l2_w2=tall(a["L2_ffn_W2"]),
        l3_w1=tall(a["L3_ffn_W1"].transpose(0, 2, 1)), l3_w2=tall(a["L3_ffn_W2"].transpose(0, 2, 1)))


def kernel(**inputs):
    import concourse.bacc as bacc
    from concourse.bass_utils import run_bass_kernel_spmd

    nc = bacc.Bacc("TRN2", target_bir_lowering=False, num_devices=1)
    arrays = arrange(inputs)
    args = [nc.dram_tensor(n, v.shape, mybir.dt.from_np(v.dtype), kind="ExternalInput").ap()
            for n, v in arrays.items()]
    args.append(nc.dram_tensor("out", (GRAPHS, P, P), F32, kind="ExternalOutput").ap())
    build(nc, *args)
    result = run_bass_kernel_spmd(nc, [arrays], core_ids=[0])
    return result.results[0]["out"]
```
